# Optimizing a Trainium2 kernel written in Bass

```python
import numpy as np
import jax
import jax.numpy as jnp

def _softmax(x, axis=-1):
    return jax.nn.softmax(x, axis=axis)

def _gelu(x):
    return jax.nn.gelu(x, approximate=True)

def _silu(x):
    return jax.nn.silu(x)

def _sigmoid(x):
    return jax.nn.sigmoid(x)

def _layernorm(x, axis=-1, eps=1e-05):
    m = jnp.mean(x, axis=axis, keepdims=True)
    v = jnp.var(x, axis=axis, keepdims=True)
    return (x - m) / jnp.sqrt(v + eps)

def _scatter_add(tgt, idx, src, axis=0):
    return tgt.at[idx].add(src)

def _segment_sum(src, seg, n):
    return jax.ops.segment_sum(src, seg, n)
kernel_name = 'mk_recurrent_d2_jaxref_r8_d990b6'

def setup_inputs(seed: int=0):
    np.random.seed(seed)
    _w = jnp.asarray

    def _L0_attn_setup():
        import jax, jax.numpy as jnp
        import numpy as np
        B, T, C, H = (8, 256, 128, 16)
        S = C // H
        LN_EPS = 1e-05
        key = jax.random.key(seed)
        ks = jax.random.split(key, 12)
        w = lambda k: jax.random.normal(k, (C, C), dtype=jnp.float32) * 0.02
        return {'x': jax.random.normal(ks[0], (B, T, C), dtype=jnp.float32), 'time_mix_k': jax.random.uniform(ks[1], (1, 1, C), dtype=jnp.float32), 'time_mix_v': jax.random.uniform(ks[2], (1, 1, C), dtype=jnp.float32), 'time_mix_r': jax.random.uniform(ks[3], (1, 1, C), dtype=jnp.float32), 'time_decay': -jax.random.uniform(ks[4], (H, S), minval=0.1, maxval=5.0, dtype=jnp.float32), 'time_first': jax.random.uniform(ks[5], (H, S), dtype=jnp.float32), 'Wk': w(ks[6]), 'Wv': w(ks[7]), 'Wr': w(ks[8]), 'Wo': w(ks[9]), 'ln_g': jnp.ones((C,), jnp.float32), 'ln_b': jnp.zeros((C,), jnp.float32)}
    _L0_attn_in = _L0_attn_setup()

    def _L0_ffn_setup():
        import jax, jax.numpy as jnp
        import numpy as np
        BLOCK = 16
        _GRID = jnp.array([0.0, 0.5, 1.0, 1.5, 2.0, 3.0, 4.0, 6.0], dtype=jnp.float32)
        _MID = jnp.array([0.25, 0.75, 1.25, 1.75, 2.5, 3.5, 5.0], dtype=jnp.float32)

        def fp4_quant_dequant(x):
            shape = x.shape
            xb = x.reshape(shape[:-1] + (shape[-1] // BLOCK, BLOCK))
            scale = jnp.max(jnp.abs(xb), axis=-1, keepdims=True) / 6.0
            scale = jnp.maximum(scale, jnp.float32(1e-12))
            xn = xb / scale
            idx = jnp.searchsorted(_MID, jnp.abs(xn))
            q = _GRID[idx] * jnp.sign(xn) * scale
            return q.reshape(shape)

        def fp4_linear(x, w):
            xq = fp4_quant_dequant(x)
            wq = fp4_quant_dequant(w)
            return jnp.einsum('bsk,nk->bsn', xq, wq)
        key = jax.random.key(seed)
        k1, k2, k3, k4 = jax.random.split(key, 4)
        H, I = (128, 352)
        x = jax.random.normal(k1, (4, 512, H), dtype=jnp.float32)
        w_gate = jax.random.normal(k2, (I, H), dtype=jnp.float32) * 0.02
        w_up = jax.random.normal(k3, (I, H), dtype=jnp.float32) * 0.02
        w_down = jax.random.normal(k4, (H, I), dtype=jnp.float32) * 0.02
        return {'x': x, 'w_gate': w_gate, 'w_up': w_up, 'w_down': w_down}
    _L0_ffn_in = _L0_ffn_setup()

    def _L1_attn_setup():
        import jax, jax.numpy as jnp
        import numpy as np
        H, D = (8, 128)
        HID = 128
        K = 4
        EPS_QK = 1e-06
        EPS_NORM = 1e-05

        def short_conv(x, w):
            k = w.shape[-1]
            xp = jnp.pad(x, ((0, 0), (k - 1, 0), (0, 0)))
            xc = jnp.transpose(xp, (0, 2, 1))
            y = jax.lax.conv_general_dilated(xc, w, window_strides=(1,), padding='VALID', feature_group_count=w.shape[0])
            return jax.nn.silu(jnp.transpose(y, (0, 2, 1)))

        def _rmsn(t, eps):
            return t * jax.lax.rsqrt(jnp.mean(t * t, axis=-1, keepdims=True) + eps)
        key = jax.random.key(seed)
        ks = jax.random.split(key, 16)
        s = 0.02
        inp = {'x': jax.random.normal(ks[0], (2, 128, HID), dtype=jnp.float32), 'Wq': jax.random.normal(ks[1], (H * D, HID), dtype=jnp.float32) * s, 'Wk': jax.random.normal(ks[2], (H * D, HID), dtype=jnp.float32) * s, 'Wv': jax.random.normal(ks[3], (H * D, HID), dtype=jnp.float32) * s, 'wq_conv': jax.random.normal(ks[4], (H * D, 1, K), dtype=jnp.float32) * 0.3, 'wk_conv': jax.random.normal(ks[5], (H * D, 1, K), dtype=jnp.float32) * 0.3, 'wv_conv': jax.random.normal(ks[6], (H * D, 1, K), dtype=jnp.float32) * 0.3, 'Wfa': jax.random.normal(ks[7], (D, HID), dtype=jnp.float32) * s, 'Wfb': jax.random.normal(ks[8], (H * D, D), dtype=jnp.float32) * s, 'Wb': jax.random.normal(ks[9], (H, HID), dtype=jnp.float32) * s, 'Wga': jax.random.normal(ks[10], (D, HID), dtype=jnp.float32) * s, 'Wgb': jax.random.normal(ks[11], (H * D, D), dtype=jnp.float32) * s, 'A_log': jnp.log(jax.random.uniform(ks[12], (H,), minval=1.0, maxval=16.0, dtype=jnp.float32)), 'dt_bias': jnp.zeros((H, D), dtype=jnp.float32), 'o_norm_w': jnp.ones((D,), dtype=jnp.float32), 'Wo': jax.random.normal(ks[13], (HID, H * D), dtype=jnp.float32) * s}
        return inp
    _L1_attn_in = _L1_attn_setup()

    def _L1_ffn_setup():
        import jax, jax.numpy as jnp
        import numpy as np
        D_MODEL = 128
        D_FF = 512
        N_EXPERTS = 4
        key = jax.random.key(seed)
        ks = jax.random.split(key, 8)
        s_in = 1.0 / np.sqrt(D_MODEL)
        s_ff = 1.0 / np.sqrt(D_FF)
        x = jax.random.normal(ks[0], (4, 256, D_MODEL), dtype=jnp.float32)
        W1 = jax.random.uniform(ks[1], (N_EXPERTS, D_MODEL, D_FF), jnp.float32, -s_in, s_in)
        b1 = jax.random.uniform(ks[2], (N_EXPERTS, D_FF), jnp.float32, -s_in, s_in)
        W2 = jax.random.uniform(ks[3], (N_EXPERTS, D_FF, D_MODEL), jnp.float32, -s_ff, s_ff)
        b2 = jax.random.uniform(ks[4], (N_EXPERTS, D_MODEL), jnp.float32, -s_ff, s_ff)
        Wg = jax.random.uniform(ks[5], (D_MODEL, N_EXPERTS), jnp.float32, -s_in, s_in)
        bg = jax.random.uniform(ks[6], (N_EXPERTS,), jnp.float32, -s_in, s_in)
        return {'x': x, 'W1': W1, 'b1': b1, 'W2': W2, 'b2': b2, 'Wg': Wg, 'bg': bg}
    _L1_ffn_in = _L1_ffn_setup()
    _d = {'L0_attn_x': _L0_attn_in['x'], 'L0_attn_time_mix_k': _L0_attn_in['time_mix_k'], 'L0_attn_time_mix_v': _L0_attn_in['time_mix_v'], 'L0_attn_time_mix_r': _L0_attn_in['time_mix_r'], 'L0_attn_time_decay': _L0_attn_in['time_decay'], 'L0_attn_time_first': _L0_attn_in['time_first'], 'L0_attn_Wk': _L0_attn_in['Wk'], 'L0_attn_Wv': _L0_attn_in['Wv'], 'L0_attn_Wr': _L0_attn_in['Wr'], 'L0_attn_Wo': _L0_attn_in['Wo'], 'L0_attn_ln_g': _L0_attn_in['ln_g'], 'L0_attn_ln_b': _L0_attn_in['ln_b'], 'L0_ffn_w_gate': _L0_ffn_in['w_gate'], 'L0_ffn_w_up': _L0_ffn_in['w_up'], 'L0_ffn_w_down': _L0_ffn_in['w_down'], 'L1_attn_Wq': _L1_attn_in['Wq'], 'L1_attn_Wk': _L1_attn_in['Wk'], 'L1_attn_Wv': _L1_attn_in['Wv'], 'L1_attn_wq_conv': _L1_attn_in['wq_conv'], 'L1_attn_wk_conv': _L1_attn_in['wk_conv'], 'L1_attn_wv_conv': _L1_attn_in['wv_conv'], 'L1_attn_Wfa': _L1_attn_in['Wfa'], 'L1_attn_Wfb': _L1_attn_in['Wfb'], 'L1_attn_Wb': _L1_attn_in['Wb'], 'L1_attn_Wga': _L1_attn_in['Wga'], 'L1_attn_Wgb': _L1_attn_in['Wgb'], 'L1_attn_A_log': _L1_attn_in['A_log'], 'L1_attn_dt_bias': _L1_attn_in['dt_bias'], 'L1_attn_o_norm_w': _L1_attn_in['o_norm_w'], 'L1_attn_Wo': _L1_attn_in['Wo'], 'L1_ffn_W1': _L1_ffn_in['W1'], 'L1_ffn_b1': _L1_ffn_in['b1'], 'L1_ffn_W2': _L1_ffn_in['W2'], 'L1_ffn_b2': _L1_ffn_in['b2'], 'L1_ffn_Wg': _L1_ffn_in['Wg'], 'L1_ffn_bg': _L1_ffn_in['bg']}
    _x0 = _d['L0_attn_x']
    _d['L0_attn_x'] = jax.random.normal(jax.random.fold_in(jax.random.key(seed), 1), (8, 1024, 128), dtype=_x0.dtype)
    del _x0
    return _d

def reference(L0_attn_x, L0_attn_time_mix_k, L0_attn_time_mix_v, L0_attn_time_mix_r, L0_attn_time_decay, L0_attn_time_first, L0_attn_Wk, L0_attn_Wv, L0_attn_Wr, L0_attn_Wo, L0_attn_ln_g, L0_attn_ln_b, L0_ffn_w_gate, L0_ffn_w_up, L0_ffn_w_down, L1_attn_Wq, L1_attn_Wk, L1_attn_Wv, L1_attn_wq_conv, L1_attn_wk_conv, L1_attn_wv_conv, L1_attn_Wfa, L1_attn_Wfb, L1_attn_Wb, L1_attn_Wga, L1_attn_Wgb, L1_attn_A_log, L1_attn_dt_bias, L1_attn_o_norm_w, L1_attn_Wo, L1_ffn_W1, L1_ffn_b1, L1_ffn_W2, L1_ffn_b2, L1_ffn_Wg, L1_ffn_bg):

    def _L0_attn_ref(x, time_mix_k, time_mix_v, time_mix_r, time_decay, time_first, Wk, Wv, Wr, Wo, ln_g, ln_b):
        import jax, jax.numpy as jnp
        import numpy as np
        B, T, C, H = (8, 256, 128, 16)
        S = C // H
        LN_EPS = 1e-05
        Bx, Tx, Cx = x.shape
        xx = jnp.pad(x, ((0, 0), (1, 0), (0, 0)))[:, :-1]
        xk = x * time_mix_k + xx * (1 - time_mix_k)
        xv = x * time_mix_v + xx * (1 - time_mix_v)
        xr = x * time_mix_r + xx * (1 - time_mix_r)
        proj = lambda z, W: jnp.einsum('btc,dc->btd', z, W).reshape(Bx, Tx, H, S)
        k = proj(xk, Wk)
        v = proj(xv, Wv)
        r = proj(xr, Wr)
        kv = k * v
        decay = jnp.exp(time_decay)

        def step(state, inp):
            kv_t, r_t = inp
            state = kv_t + decay * state
            o = r_t * (time_first * kv_t + state)
            return (state, o)
        kvT = jnp.swapaxes(kv, 0, 1)
        rT = jnp.swapaxes(r, 0, 1)
        _, outT = jax.lax.scan(step, jnp.zeros((Bx, H, S), x.dtype), (kvT, rT))
        out = jnp.swapaxes(outT, 0, 1).reshape(Bx, Tx, Cx)
        mu = out.mean(-1, keepdims=True)
        var = out.var(-1, keepdims=True)
        out = (out - mu) / jnp.sqrt(var + LN_EPS) * ln_g + ln_b
        return jnp.einsum('btc,dc->btd', out, Wo)

    def _L0_ffn_ref(x, w_gate, w_up, w_down):
        import jax, jax.numpy as jnp
        import numpy as np
        BLOCK = 16
        _GRID = jnp.array([0.0, 0.5, 1.0, 1.5, 2.0, 3.0, 4.0, 6.0], dtype=jnp.float32)
        _MID = jnp.array([0.25, 0.75, 1.25, 1.75, 2.5, 3.5, 5.0], dtype=jnp.float32)

        def fp4_quant_dequant(x):
            shape = x.shape
            xb = x.reshape(shape[:-1] + (shape[-1] // BLOCK, BLOCK))
            scale = jnp.max(jnp.abs(xb), axis=-1, keepdims=True) / 6.0
            scale = jnp.maximum(scale, jnp.float32(1e-12))
            xn = xb / scale
            idx = jnp.searchsorted(_MID, jnp.abs(xn))
            q = _GRID[idx] * jnp.sign(xn) * scale
            return q.reshape(shape)

        def fp4_linear(x, w):
            xq = fp4_quant_dequant(x)
            wq = fp4_quant_dequant(w)
            return jnp.einsum('bsk,nk->bsn', xq, wq)
        gate = fp4_linear(x, w_gate)
        y = fp4_linear(x, w_up)
        h = jax.nn.silu(gate) * y
        return fp4_linear(h, w_down)

    def _L1_attn_ref(x, Wq, Wk, Wv, wq_conv, wk_conv, wv_conv, Wfa, Wfb, Wb, Wga, Wgb, A_log, dt_bias, o_norm_w, Wo):
        import jax, jax.numpy as jnp
        import numpy as np
        H, D = (8, 128)
        HID = 128
        K = 4
        EPS_QK = 1e-06
        EPS_NORM = 1e-05

        def short_conv(x, w):
            k = w.shape[-1]
            xp = jnp.pad(x, ((0, 0), (k - 1, 0), (0, 0)))
            xc = jnp.transpose(xp, (0, 2, 1))
            y = jax.lax.conv_general_dilated(xc, w, window_strides=(1,), padding='VALID', feature_group_count=w.shape[0])
            return jax.nn.silu(jnp.transpose(y, (0, 2, 1)))

        def _rmsn(t, eps):
            return t * jax.lax.rsqrt(jnp.mean(t * t, axis=-1, keepdims=True) + eps)
        B, T, _ = x.shape
        scale = float(D) ** (-0.5)
        q = short_conv(x @ Wq.T, wq_conv).reshape(B, T, H, D)
        k = short_conv(x @ Wk.T, wk_conv).reshape(B, T, H, D)
        v = short_conv(x @ Wv.T, wv_conv).reshape(B, T, H, D)
        q = scale ** 2 * _rmsn(q, EPS_QK)
        k = scale * _rmsn(k, EPS_QK)
        a_logits = (x @ Wfa.T @ Wfb.T).reshape(B, T, H, D)
        g = -jnp.exp(A_log)[None, None, :, None] * jax.nn.softplus(a_logits + dt_bias)
        beta = jax.nn.sigmoid(x @ Wb.T)

        def step(S, inputs):
            q_t, k_t, v_t, g_t, b_t = inputs
            S = S * jnp.exp(g_t)[..., None]
            kv = jnp.einsum('bhd,bhdv->bhv', k_t, S)
            delta = b_t[..., None] * (v_t - kv)
            S = S + k_t[..., None] * delta[:, :, None, :]
            o = jnp.einsum('bhd,bhdv->bhv', q_t, S)
            return (S, o)
        tb = lambda t: jnp.moveaxis(t, 1, 0)
        S0 = jnp.zeros((B, H, D, D), dtype=x.dtype)
        _, o_t = jax.lax.scan(step, S0, (tb(q), tb(k), tb(v), tb(g), tb(beta)))
        out = jnp.moveaxis(o_t, 0, 1)
        gate = (x @ Wga.T @ Wgb.T).reshape(B, T, H, D)
        out = _rmsn(out, EPS_NORM) * o_norm_w * jax.nn.sigmoid(gate)
        return out.reshape(B, T, H * D) @ Wo.T

    def _L1_ffn_ref(x, W1, b1, W2, b2, Wg, bg):
        import jax, jax.numpy as jnp
        import numpy as np
        D_MODEL = 128
        D_FF = 512
        N_EXPERTS = 4
        gate_logits = jnp.einsum('bld,de->ble', x, Wg) + bg
        idx = jnp.argmax(jax.nn.softmax(gate_logits, axis=-1), axis=-1)
        h = jnp.einsum('bld,edf->belf', x, W1) + b1[None, :, None, :]
        h = jax.nn.gelu(h, approximate=False)
        y = jnp.einsum('belf,efd->beld', h, W2) + b2[None, :, None, :]
        onehot = jax.nn.one_hot(idx, N_EXPERTS, dtype=x.dtype)
        out = jnp.einsum('beld,ble->bld', y, onehot)
        return out
    x = L0_attn_x
    xn = _layernorm(x, axis=-1)
    s = _L0_attn_ref(xn, L0_attn_time_mix_k, L0_attn_time_mix_v, L0_attn_time_mix_r, L0_attn_time_decay, L0_attn_time_first, L0_attn_Wk, L0_attn_Wv, L0_attn_Wr, L0_attn_Wo, L0_attn_ln_g, L0_attn_ln_b)
    g = _silu(_L0_ffn_ref(xn, L0_ffn_w_gate, L0_ffn_w_up, L0_ffn_w_down))
    x = x + s * g
    xn = _layernorm(x, axis=-1)
    s = _L1_attn_ref(xn, L1_attn_Wq, L1_attn_Wk, L1_attn_Wv, L1_attn_wq_conv, L1_attn_wk_conv, L1_attn_wv_conv, L1_attn_Wfa, L1_attn_Wfb, L1_attn_Wb, L1_attn_Wga, L1_attn_Wgb, L1_attn_A_log, L1_attn_dt_bias, L1_attn_o_norm_w, L1_attn_Wo)
    g = _silu(_L1_ffn_ref(xn, L1_ffn_W1, L1_ffn_b1, L1_ffn_W2, L1_ffn_b2, L1_ffn_Wg, L1_ffn_bg))
    x = x + s * g
    return x

_drawn_inputs = setup_inputs


def setup_inputs(seed=0):
    import zlib

    import numpy as np

    out = dict(_drawn_inputs(seed))
    spreads = {'L0_attn_ln_g': (1.0, 0.6),
     'L0_attn_ln_b': (0.0, 0.8),
     'L1_attn_dt_bias': (0.0, 2.0),
     'L1_attn_o_norm_w': (1.0, 0.6)}
    factors = {'L0_attn_time_mix_k': 8.0,
     'L0_attn_time_mix_v': 8.0,
     'L0_attn_time_mix_r': 8.0,
     'L0_attn_time_decay': 8.0,
     'L0_attn_time_first': 8.0,
     'L0_attn_Wk': 8.0,
     'L0_attn_Wv': 8.0,
     'L0_attn_Wr': 8.0,
     'L0_attn_Wo': 8.0,
     'L0_ffn_w_gate': 8.0,
     'L0_ffn_w_up': 8.0,
     'L0_ffn_w_down': 8.0,
     'L1_attn_Wq': 8.0,
     'L1_attn_Wk': 8.0,
     'L1_attn_Wv': 8.0,
     'L1_attn_wq_conv': 8.0,
     'L1_attn_wk_conv': 8.0,
     'L1_attn_wv_conv': 8.0,
     'L1_attn_Wfa': 8.0,
     'L1_attn_Wfb': 8.0,
     'L1_attn_Wb': 8.0,
     'L1_attn_Wga': 8.0,
     'L1_attn_Wgb': 8.0,
     'L1_attn_A_log': 8.0,
     'L1_attn_Wo': 8.0,
     'L1_ffn_W1': 8.0,
     'L1_ffn_b1': 8.0,
     'L1_ffn_W2': 8.0,
     'L1_ffn_b2': 35.029,
     'L1_ffn_Wg': 8.0,
     'L1_ffn_bg': 8.0}
    for name, (base, spread) in spreads.items():
        noise = np.random.default_rng([zlib.crc32(name.encode()), seed]).standard_normal(out[name].shape)
        drawn = base * np.exp(spread * noise) if base else spread * noise
        out[name] = jnp.asarray(drawn.astype(out[name].dtype))
    for name, factor in factors.items():
        out[name] = (out[name] * factor).astype(out[name].dtype)
    return out
```

```python
import concourse.bass as bass
from concourse import mybir
from contextlib import ExitStack

F32 = mybir.dt.float32
U32 = mybir.dt.uint32
ALU = mybir.AluOpType
ACT = mybir.ActivationFunctionType

P = 128
T = 1024
XS = T + 1
B = 8
H1 = 8
CH = T // P
TAPS = 4
LEVELS = 7
HALF = 512
ITEMS = B * H1

W_A, W_K, W_Q, W_V, W_G = (P * n for n in range(5))
W_TAPS = 5 * P
W_DT = W_TAPS + 3 * TAPS
W_NEGA = W_DT + 1
W_O = W_NEGA + 3
PACK = W_O + P

Q_EPS, K_EPS, O_EPS = 1e-6, 1e-6, 1e-5


def halves(level):
    h = 1 << level
    return h, T // (2 * h)


def first(ap, level):
    h = 1 << level
    return ap.rearrange("p (n t) -> p n t", t=2 * h)[:, :, 0:h]


def second(ap, level):
    h = 1 << level
    return ap.rearrange("p (n t) -> p n t", t=2 * h)[:, :, h:2 * h]


def each(ap, n):
    return ap.unsqueeze(2).to_broadcast([P, ap.shape[1], n])


AHEAD = 2


class Counters:

    def __init__(self, nc, ctx, prefix=""):
        self.nc, self.ctx, self.prefix, self.per, self.all = nc, ctx, prefix, {}, []

    def sem(self, name, per_item):
        s = self.ctx.enter_context(self.nc.semaphore(self.prefix + name))
        self.per[s.name] = per_item
        self.all.append(s)
        return s

    def upto(self, s, item, k=None):
        n = self.per[s.name]
        return (item + AHEAD) * n + (n if k is None else k)

    def start(self, eng):
        for s in self.all:
            if self.per[s.name]:
                eng.sem_inc(s, AHEAD * self.per[s.name])



def l1_attention(nc, xn, s_acc, beta, ident, ones_mean, masks_a, masks_x, wscr):
    with ExitStack() as ctx:
        def sb(name, cols, dt=F32):
            return ctx.enter_context(nc.sbuf_tensor(name, [P] + list(cols), dt))

        xs = sb("xs", [2, T])
        pack = sb("pack", [2, W_O])
        wop = sb("wop", [2, P])
        raw = sb("raw", [2, 3 + T])
        ks = sb("ks", [2, T])
        cq = sb("cq", [T])
        cv = sb("cv", [T])
        at = sb("at", [T])
        ar = sb("ar", [T])
        al = sb("al", [T])
        aw = sb("aw", [T])
        dec = sb("dec", [T])
        small = sb("small", [4, CH])
        gam = sb("gam", [CH])
        mg = sb("mg", [T // 2])
        etot = sb("etot", [CH])
        halfc, epsc = sb("halfc", [CH]), sb("epsc", [1])
        kq = sb("kq", [2, 2, T])
        gt = sb("gt", [2, T])
        q2 = sb("q2", [2, T])
        akk = sb("akk", [T])
        aqk = sb("aqk", [2, T])
        kst = sb("kst", [2, T])
        vs = sb("vs", [2, T])
        gm = sb("gm", [T])
        gmt = sb("gmt", [2, T])
        xb = sb("xb", [3, T])
        st = sb("st", [CH, P])
        rt = sb("rt", [P])
        dl = sb("dl", [CH, P])
        osb = sb("osb", [T])
        o2 = sb("o2", [T])

        bank = [ctx.enter_context(nc.psum_tensor(f"bank{n}", [P, HALF], F32)) for n in range(8)]
        b_x = bank[0:2]
        b_sum = bank[1][:, HALF // 2:]
        b_l = bank[2:4]
        b_g = bank[4:6]
        b_c, b_m = b_o = bank[6:8]

        counters = Counters(nc, ctx)
        sem, upto = counters.sem, counters.upto
        init_done = sem("init_done", 0)
        cleared = sem("cleared", 0)
        passed = sem("passed", 0)
        x_in = [sem(f"x_in{p}", 16) for p in range(2)]
        pack_in = [sem(f"pack_in{p}", 16) for p in range(2)]
        wo_in = [sem(f"wo_in{p}", 16) for p in range(2)]
        proj = sem("proj", 8)
        evac = sem("evac", 8)
        gproj = sem("gproj", 2)
        gact = sem("gact", 2)
        absz = sem("absz", 2)
        texp = sem("texp", 1)
        tln = sem("tln", 1)
        wround = sem("wround", 1)
        wcorr = sem("wcorr", 1)
        splus = sem("splus", 2)
        adone = sem("adone", 1)
        conv = sem("conv", 12)
        silu = sem("silu", 3)
        sqr = sem("sqr", 2)
        qk = sem("qk", 1)
        kqd = sem("kqd", 2)
        sums = sem("sums", 1)
        stat = sem("stat", 4)
        knorm = sem("knorm", 1)
        ginit = sem("ginit", 1)
        tinit = sem("tinit", 1)
        mginit = sem("mginit", 1)
        diag = sem("diag", 1)
        vtr = sem("vtr", 2)
        vsd = sem("vsd", 2)
        lprod = sem("lprod", 2 * LEVELS)
        kcopy = sem("kcopy", 2 * LEVELS)
        qcopy = sem("qcopy", 2 * LEVELS)
        lup = sem("lup", 4 * LEVELS)
        ktr = sem("ktr", 2)
        ktd = sem("ktd", 2)
        xprod = sem("xprod", 2 * LEVELS)
        xcopy = sem("xcopy", 2 * LEVELS)
        gprod = sem("gprod", 2 * LEVELS - 2)
        gsub = sem("gsub", 2 * LEVELS - 2)
        gturn = sem("gturn", 2 * LEVELS - 2)
        tcopy = sem("tcopy", 2 * LEVELS - 2)
        tlast = sem("tlast", 2)
        rprod = sem("rprod", 7)
        rsub = sem("rsub", 7)
        dprod = sem("dprod", 8)
        dcopy = sem("dcopy", 8)
        sprod = sem("sprod", 7)
        snew = sem("snew", 7)
        oprod = sem("oprod", 2)
        ocopy = sem("ocopy", 2)
        osq = sem("osq", 2)
        oq2 = sem("oq2", 2)
        osum = sem("osum", 2)
        oln = sem("oln", 2)
        orstd = sem("orstd", 2)
        ogate = sem("ogate", 4)
        wo = sem("wo", 2)
        sacc = sem("sacc", 2)

        turn = """L0a L0b C0d X0a C0s X0b C1r G0a Pa G0b C1d Ba L1a C1s Y0a C2r L1b C2d Y0b Ue
            X1a C2s X1b G1a C3r G1b C3d Ul Pk E C3s L2a C4r Y1a L2b C4d Y1b F
            X2a C4s X2b G2a C5r T00 G2b C5d Pq T01 C5s L3a C6r Y2a L3b T02 C6d Sv Y2b
            X3a C6s X3b Va G3a C7r T03 G3b C7d Pv T10 Sk L4a Vb Y3a T11 L4b Y3b Pg T12
            X4a Z Oa X4b T13 G4a Ob Sq G4b T20 L5a Y4a T21 L5b Y4b T22
            X5a Na X5b T23 Nb G5a D Q G5b M0 L6a Ra M1 Y5a L6b Rb M2 Y5b M3 J
            X6a Wa X6b Wb I G6a G6b Ka Kb""".split()

        def turns(eng, step):
            def steps(i, p, before=True, behind=True, own=True):
                for s in turn:
                    if s[0] in "CONRW":
                        if before:
                            step(s, i - 1, 1 - p)
                    elif s in ("Pg", "Sv") or s[0] in "LXGYKV":
                        if own:
                            step(s, i, p)
                    elif behind:
                        step(s, i + 1, 1 - p)
            steps(-1, 1, before=False, own=False)
            steps(0, 0, before=False)
            with eng.Fori(0, ITEMS // 2 - 1) as j:
                steps(2 * j + 1, 1)
                steps(2 * j + 2, 0)
            steps(ITEMS - 1, 1, behind=False)
            steps(ITEMS, 0, behind=False, own=False)

        def is_last(i, n=1):
            return isinstance(i, int) and i == ITEMS - n

        block = ctx.enter_context(nc.Block())

        @block.sync
        def _(sp):
            counters.start(sp)

            def load(i, p):
                sp.wait_ge(gproj, upto(gproj, i - 2))
                sp.sem_inc(passed, 1)
                sp.dma_start(xs[:, p, :], xn.rearrange("p (b t) -> b p t", t=T)[i // H1]).then_inc(x_in[p], 16)
                sp.wait_ge(conv, upto(conv, i - 2))
                sp.sem_inc(passed, 1)
                sp.wait_ge(adone, upto(adone, i - 2))
                sp.sem_inc(passed, 1)
                sp.dma_start(pack[:, p, :], wscr[i % H1, :, 0:W_O]).then_inc(pack_in[p], 16)
                sp.wait_ge(wo, upto(wo, i - 2))
                sp.sem_inc(passed, 1)
                sp.dma_start(wop[:, p, :], wscr[i % H1, :, W_O:W_O + P]).then_inc(wo_in[p], 16)

            load(0, 0)
            load(1, 1)
            with sp.Fori(0, ITEMS // 2 - 1) as j:
                load(2 * j + 2, 0)
                load(2 * j + 3, 1)

        def chunk(ap, c):
            return ap[:, c * P:(c + 1) * P]

        def cols(half):
            return slice(half * HALF, (half + 1) * HALF)

        def level(s):
            return int(s[1]), "ab".index(s[2])

        def other(s):
            return "ab".index(s[1])

        @block.tensor
        def _(pe):
            def mm(out, lhsT, rhs, start=True, stop=True):
                return nc.tensor.matmul(out, lhsT, rhs, start=start, stop=stop)

            def turn_chunks(out, src, half):
                for g in range(4):
                    last = nc.tensor.transpose(chunk(out, g), chunk(src, 4 * half + g), ident)
                return last

            def step(s, i, p):
                if s == "Pg":
                    pe.wait_ge(dcopy, upto(dcopy, i - 1))
                    pe.wait_ge(vsd, upto(vsd, i))
                    for half in range(2):
                        mm(b_o[half][:], pack[:, p, W_G:W_G + P], xs[:, p, cols(half)]).then_inc(gproj, 1)
                elif s[0] == "P":
                    j = "akqv".index(s[1])
                    col = (W_A, W_K, W_Q, W_V)[j]
                    if j == 0:
                        pe.wait_ge(pack_in[p], upto(pack_in[p], i // 2))
                        pe.wait_ge(x_in[p], upto(x_in[p], i // 2))
                    for half in range(2):
                        if j:
                            pe.wait_ge(evac, upto(evac, i, 2 * j + half - 1))
                        else:
                            pe.wait_ge(xcopy, upto(xcopy, i - 1, half + 1))
                        mm(b_x[half][:], pack[:, p, col:col + P], xs[:, p, cols(half)]).then_inc(proj, 1)
                if s[0] == "M":
                    k = int(s[1])
                    if k == 0:
                        pe.wait_ge(sqr, upto(sqr, i, 1))
                    if k == 2:
                        pe.wait_ge(qk, upto(qk, i))
                    for g in range(4):
                        c = 4 * k + g
                        last = mm(b_sum[:, c:c + 1], chunk((at, ar)[k // 2], c % CH), ones_mean[:, 0:1])
                    if k == 3:
                        last.then_inc(sums, 1)
                if s[0] == "V":
                    half = other(s)
                    if half == 0:
                        pe.wait_ge(silu, upto(silu, i))
                        pe.wait_ge(ktd, upto(ktd, i - 1))
                    else:
                        pe.wait_ge(vsd, upto(vsd, i, 1))
                    turn_chunks(b_m, cv, half).then_inc(vtr, 1)
                if s[0] == "L":
                    l, half = level(s)
                    h, _ = halves(l)
                    nb = P // (2 * h)
                    if l == 0:
                        pe.wait_ge(kqd, upto(kqd, i))
                    else:
                        pe.wait_ge(lup, upto(lup, i, 4 * l - 1))
                    pe.wait_ge(kcopy, upto(kcopy, i, 2 * l + half - 1))
                    pe.wait_ge(qcopy, upto(qcopy, i, 2 * l + half - 1))
                    for g in range(4):
                        c = 4 * half + g
                        rhs = kq[:, p].rearrange("p two (n t) -> p two n t", t=2 * h)[:, :, c * nb:(c + 1) * nb, h:2 * h]
                        last = mm(chunk(b_l[half], g), chunk(ks[:, p, :], c), rhs)
                    last.then_inc(lprod, 1)
                if s[0] == "K":
                    half = other(s)
                    pe.wait_ge(lup, upto(lup, i))
                    pe.wait_ge(gact, upto(gact, i))
                    pe.wait_ge(sacc, upto(sacc, i - 1, half + 1))
                    turn_chunks(b_o[half], ks[:, p, :], half).then_inc(ktr, 1)
                if s[0] == "X":
                    l, half = level(s)
                    if l == 0:
                        pe.wait_ge(ginit, upto(ginit, i))
                    else:
                        pe.wait_ge(gsub, upto(gsub, i, 2 * l - 1 + half))
                    if l in (1, 2, 3, 4) and not is_last(i):
                        pe.wait_ge(evac, upto(evac, i + 1, 2 * l - 1 + half))
                    if l == 6 and half and not is_last(i):
                        pe.wait_ge(stat, upto(stat, i + 1, 2))
                    pe.wait_ge(kcopy, upto(kcopy, i, 2 * l + half + 1))
                    for g in range(4):
                        c = 4 * half + g
                        last = mm(b_x[half][:, g * 64:(g + 1) * 64], chunk(akk, c), first(chunk(gm, c), l))
                    last.then_inc(xprod, 1)
                if s[0] == "G" and s[1] != "0":
                    l, half = level(s)
                    pe.wait_ge(xcopy, upto(xcopy, i, 2 * l + half + 1))
                    pe.wait_ge(tcopy, upto(tcopy, i, 2 * l - 1 + half))
                    for g in range(4):
                        c = 4 * half + g
                        if l < LEVELS - 1:
                            last = mm(b_g[half][:, g * 64:(g + 1) * 64], chunk(gmt[:, p, :], c),
                                      first(chunk(xb[:, l % 2, :], c), l))
                        else:
                            last = mm(b_g[half][:, g * 64:(g + 1) * 64], chunk(xb[:, 2, :], c),
                                      second(chunk(gmt[:, p, :], c), l))
                    last.then_inc(gprod, 1)
                if s[0] == "Y":
                    l, half = level(s)
                    pe.wait_ge(gsub, upto(gsub, i, 2 * l + half + 1))
                    if l == 0:
                        pe.wait_ge(tlast, upto(tlast, i - 1, half + 1))
                    for g in range(4):
                        last = nc.tensor.transpose(chunk(b_g[half], g), chunk(gm, 4 * half + g), ident)
                    last.then_inc(gturn, 1)
                if s[0] == "C":
                    c = int(s[1])
                    if s[2] == "r" and c:
                        pe.wait_ge(snew, upto(snew, i, c))
                        mm(b_c[:, 0:P], chunk(kq[:, p, 0, :], c), st[:, c, :]).then_inc(rprod, 1)
                    if s[2] == "d":
                        if c == 0:
                            pe.wait_ge(tlast, upto(tlast, i))
                            pe.wait_ge(vsd, upto(vsd, i))
                            pe.wait_ge(ktd, upto(ktd, i))
                            pe.wait_ge(sacc, upto(sacc, i - 1))
                            mm(b_c[:, 0:P], chunk(gmt[:, p, :], c), chunk(vs[:, p, :], 0)).then_inc(dprod, 1)
                        else:
                            pe.wait_ge(rsub, upto(rsub, i, c))
                            mm(b_c[:, 0:P], chunk(gmt[:, p, :], c), rt[:]).then_inc(dprod, 1)
                    if s[2] == "s":
                        pe.wait_ge(dcopy, upto(dcopy, i, c + 1))
                        mm(b_c[:, 0:P], chunk(kst[:, p, :], c), dl[:, c, :]).then_inc(sprod, 1)
                if s[0] == "O":
                    half = other(s)
                    pe.wait_ge(dcopy, upto(dcopy, i))
                    pe.wait_ge(qcopy, upto(qcopy, i))
                    if not is_last(i):
                        pe.wait_ge(gact, upto(gact, i + 1, half + 1))
                    for g in range(4):
                        c = 4 * half + g
                        out = chunk(b_o[half], g)
                        if c:
                            mm(out, st[:, c, :], chunk(kq[:, p, 1, :], c), stop=False)
                        last = mm(out, dl[:, c, :], chunk(aqk[:, p, :], c), start=(c == 0))
                    last.then_inc(oprod, 1)
                if s[0] == "N":
                    half = other(s)
                    pe.wait_ge(oq2, upto(oq2, i, half + 1))
                    pe.wait_ge(ocopy, upto(ocopy, i, half + 1))
                    mm(b_o[half][:], ones_mean, o2[:, cols(half)]).then_inc(osum, 1)
                if s[0] == "W":
                    half = other(s)
                    pe.wait_ge(ogate, upto(ogate, i, 2 * half + 2))
                    pe.wait_ge(wo_in[p], upto(wo_in[p], i // 2))
                    mm(b_o[half][:], wop[:, p, :], osb[:, cols(half)]).then_inc(wo, 1)

            pe.wait_ge(init_done, 3)
            turns(pe, step)

        @block.scalar
        def _(act):
            A = nc.scalar.activation

            def step(s, i, p):
                if s == "Ba":
                    act.wait_ge(pack_in[p], upto(pack_in[p], i // 2))
                    act.wait_ge(sums, upto(sums, i - 1))
                    z = pack[:, p, W_DT:W_DT + 1]
                    for half in range(2):
                        act.wait_ge(proj, upto(proj, i, half + 1))
                        A(at[:, cols(half)], b_x[half][:], ACT.Abs, bias=z).then_inc(absz, 1)
                        A(ar[:, cols(half)], b_x[half][:], ACT.Relu, bias=z).then_inc(evac, 1)
                elif s == "Pg":
                    act.wait_ge(ogate, upto(ogate, i - 2))
                    for half in range(2):
                        act.wait_ge(gproj, upto(gproj, i, half + 1))
                        A(gt[:, p, cols(half)], b_o[half][:], ACT.Tanh, scale=0.5).then_inc(gact, 1)
                elif s[0] == "P" and s[1] in "kqv":
                    t = "kqv".index(s[1])
                    act.wait_ge(conv, upto(conv, i, 4 * (t - 1)))
                    for half in range(2):
                        act.wait_ge(proj, upto(proj, i, 2 * t + half + 3))
                        A(raw[:, t % 2, 3 + half * HALF:3 + (half + 1) * HALF], b_x[half][:],
                          ACT.Copy).then_inc(evac, 1)
                if s == "Ue":
                    act.wait_ge(absz, upto(absz, i))
                    A(at[:], at[:], ACT.Exp, scale=-1.0).then_inc(texp, 1)
                if s == "Ul":
                    act.wait_ge(texp, upto(texp, i))
                    act.wait_ge(lup, upto(lup, i - 1, 4))
                    act.wait_ge(kqd, upto(kqd, i - 1))
                    A(al[:], at[:], ACT.Ln, bias=1.0).then_inc(tln, 1)
                if s == "F":
                    act.wait_ge(splus, upto(splus, i))
                    A(al[:], al[:], ACT.Exp, scale=pack[:, p, W_NEGA:W_NEGA + 1]).then_inc(adone, 1)
                if s == "Sk":
                    act.wait_ge(conv, upto(conv, i, 4))
                    A(ks[:, p, :], ks[:, p, :], ACT.Silu).then_inc(silu, 1)
                if s == "Z":
                    act.wait_ge(silu, upto(silu, i, 1))
                    act.wait_ge(wcorr, upto(wcorr, i))
                    A(at[:], ks[:, p, :], ACT.Square).then_inc(sqr, 1)
                if s == "Sq":
                    act.wait_ge(conv, upto(conv, i, 8))
                    A(cq[:], cq[:], ACT.Silu).then_inc(silu, 1)
                if s == "Q":
                    act.wait_ge(silu, upto(silu, i, 2))
                    act.wait_ge(oq2, upto(oq2, i - 2))
                    A(q2[:, p, :], cq[:], ACT.Square, scale=float((O_EPS * P * P) ** 0.5)).then_inc(sqr, 1)
                if s == "Sv":
                    act.preload_act_table_set("silu_and_others")
                    act.wait_ge(conv, upto(conv, i))
                    A(cv[:], cv[:], ACT.Silu).then_inc(silu, 1)
                if s[0] == "K":
                    half = other(s)
                    act.wait_ge(ktr, upto(ktr, i, half + 1))
                    act.wait_ge(sprod, upto(sprod, i - 2))
                    A(kst[:, p, cols(half)], b_o[half][:], ACT.Copy).then_inc(ktd, 1)
                if s[0] == "C" and s[2] == "d":
                    c = int(s[1])
                    act.wait_ge(dprod, upto(dprod, i, c + 1))
                    act.wait_ge(oprod, upto(oprod, i - 1))
                    A(dl[:, c, :], b_c[:, 0:P], ACT.Copy).then_inc(dcopy, 1)
                if s[0] == "O":
                    half = other(s)
                    act.wait_ge(oprod, upto(oprod, i, half + 1))
                    act.wait_ge(ogate, upto(ogate, i - 1))
                    A(o2[:, cols(half)], b_o[half][:], ACT.Square).then_inc(osq, 1)
                    act.wait_ge(wo, upto(wo, i - 1))
                    A(osb[:, cols(half)], b_o[half][:], ACT.Copy).then_inc(ocopy, 1)
                if s[0] == "Y":
                    l, half = level(s)
                    act.wait_ge(gturn, upto(gturn, i, 2 * l + half + 1))
                    if l == 0:
                        act.wait_ge(tinit, upto(tinit, i))
                    A(second(gmt[:, p, cols(half)], l), second(b_g[half][:], l), ACT.Copy).then_inc(tcopy, 1)
                if s[0] == "N":
                    half = other(s)
                    if half == 0:
                        act.preload_act_table_set("natural_log_exp_and_others")
                    act.wait_ge(osum, upto(osum, i, half + 1))
                    A(o2[:, cols(half)], b_o[half][:], ACT.Ln, bias=epsc[:, 0:1]).then_inc(oln, 1)
                    act.wait_ge(oln, upto(oln, i, half + 1))
                    A(o2[:, cols(half)], o2[:, cols(half)], ACT.Exp, scale=-0.5).then_inc(orstd, 1)

            act.preload_act_table_set("natural_log_exp_and_others")
            act.wait_ge(init_done, 3)
            turns(act, step)

        @block.vector
        def _(dve):
            V = nc.vector
            V.memset(raw[:], 0.0).then_inc(init_done, 1)
            V.memset(epsc[:], float(O_EPS * P * P * Q_EPS))
            V.memset(halfc[:], 0.5).then_inc(init_done, 1)

            def by_chunk(ap):
                return ap.rearrange("p (g v) -> p g v", v=P)

            def level_copy(dst, src, t, l, half):
                h, _ = halves(l)
                dst = dst[:, cols(half)].rearrange("p (g n t) -> p g n t", g=4, t=2 * h)[:, :, :, h:2 * h]
                src = src[:].rearrange("p (g two n t) -> p g two n t", g=4, two=2, t=h)[:, :, t]
                mask = masks_a[:, l, :].rearrange("p (n t) -> p n t", t=h).unsqueeze(1).to_broadcast([P, 4, 64 // h, h])
                dve.sem_inc(passed, 1)
                return V.copy_predicated(dst, mask.bitcast(U32), src)

            def step(s, i, p):
                if s == "E":
                    dve.wait_ge(texp, upto(texp, i))
                    dve.wait_ge(splus, upto(splus, i - 1))
                    V.tensor_scalar(aw[:], at[:], 1.0, 1.0, ALU.add, ALU.subtract).then_inc(wround, 1)
                    dve.wait_ge(wround, upto(wround, i))
                    V.tensor_tensor(aw[:], at[:], aw[:], ALU.subtract).then_inc(wcorr, 1)
                if s[0] == "T":
                    t, n = int(s[1]), int(s[2])
                    tap = TAPS - 1 - n
                    w = pack[:, p, W_TAPS + TAPS * t + tap:W_TAPS + TAPS * t + tap + 1]
                    src, dst = raw[:, t % 2, tap:tap + T], (ks[:, p, :], cq[:], cv[:])[t]
                    if n == 0:
                        dve.wait_ge(pack_in[p], upto(pack_in[p], i // 2))
                        dve.wait_ge(evac, upto(evac, i, 2 * t + 4))
                        if t == 0:
                            dve.wait_ge(ktr, upto(ktr, i - 2))
                        if t == 1:
                            dve.wait_ge(sqr, upto(sqr, i - 1))
                            dve.wait_ge(qk, upto(qk, i - 1))
                            dve.wait_ge(kqd, upto(kqd, i - 1))
                        if t == 2:
                            dve.wait_ge(vtr, upto(vtr, i - 1))
                        V.tensor_scalar(dst, src, w, None, ALU.mult).then_inc(conv, 1)
                    else:
                        dve.wait_ge(conv, upto(conv, i, 4 * t + n))
                        V.scalar_tensor_tensor(dst, src, w, dst, ALU.mult, ALU.add).then_inc(conv, 1)
                if s == "D":
                    dve.wait_ge(oprod, upto(oprod, i - 2))
                    dve.wait_ge(adone, upto(adone, i))
                    dve.wait_ge(silu, upto(silu, i, 2))
                    V.tensor_tensor(kq[:, p, 0, :], ks[:, p, :], al[:], ALU.mult).then_inc(kqd, 1)
                    V.tensor_tensor(kq[:, p, 1, :], cq[:], al[:], ALU.mult).then_inc(kqd, 1)
                if s == "M3":
                    dve.wait_ge(sums, upto(sums, i))
                    dve.wait_ge(diag, upto(diag, i - 1))
                    dve.wait_ge(vsd, upto(vsd, i - 1))
                    V.tensor_scalar(small[:, 0, :], b_sum[:, 0:CH], float(P), float(P * K_EPS), ALU.mult, ALU.add).then_inc(stat, 1)
                    V.tensor_scalar(small[:, 1, :], b_sum[:, CH:2 * CH], float(P), None, ALU.mult).then_inc(stat, 1)
                    dve.wait_ge(stat, upto(stat, i, 1))
                    V.reciprocal(small[:, 2, :], small[:, 0, :]).then_inc(stat, 1)
                    dve.wait_ge(stat, upto(stat, i, 3))
                    dve.wait_ge(tinit, upto(tinit, i - 1))
                    dve.wait_ge(mginit, upto(mginit, i - 1))
                    dve.wait_ge(ginit, upto(ginit, i - 1))
                    V.tensor_tensor(gam[:], small[:, 2, :], beta[:, bass.ds(i * CH, CH)], ALU.mult).then_inc(stat, 1)
                if s[0] == "V":
                    half = other(s)
                    dve.wait_ge(knorm, upto(knorm, i))
                    dve.wait_ge(dprod, upto(dprod, i - 2))
                    dve.wait_ge(vtr, upto(vtr, i, half + 1))
                    V.tensor_tensor(by_chunk(vs[:, p, cols(half)]), by_chunk(b_m[:]),
                                    each(small[:, 3, 4 * half:4 * half + 4], P), ALU.mult).then_inc(vsd, 1)
                if s == "I":
                    dve.wait_ge(stat, upto(stat, i))
                    dve.wait_ge(xprod, upto(xprod, i - 1))
                    V.tensor_tensor(by_chunk(gm[:]), ident.unsqueeze(1).to_broadcast([P, CH, P]),
                                    each(gam[:], P), ALU.mult).then_inc(ginit, 1)
                if s[0] == "L":
                    l, half = level(s)
                    dve.wait_ge(lprod, upto(lprod, i, 2 * l + half + 1))
                    level_copy(akk, b_l[half], 0, l, half).then_inc(kcopy, 1)
                if s[0] == "X":
                    l, half = level(s)
                    h, _ = halves(l)
                    dve.wait_ge(xprod, upto(xprod, i, 2 * l + half + 1))
                    if l in (0, 1, LEVELS - 1):
                        dve.wait_ge(gprod, upto(gprod, i - 1))
                    elif l == 2:
                        dve.wait_ge(gsub, upto(gsub, i, half + 1))
                    else:
                        dve.wait_ge(gprod, upto(gprod, i, 2 * l - 5 + half))
                    x = xb[:, 2 if l == LEVELS - 1 else l % 2, cols(half)]
                    if l == 0:
                        dve.wait_ge(mginit, upto(mginit, i))
                        mask = mg[:, half * 256:(half + 1) * 256].unsqueeze(2)
                    else:
                        mask = masks_x[:, l, :].unsqueeze(1).to_broadcast([P, 4, 64])
                    V.tensor_tensor(first(x, l), b_x[half][:, 0:256].rearrange("p (n t) -> p n t", t=h),
                                    mask, ALU.mult).then_inc(xcopy, 1)
                    dve.wait_ge(diag, upto(diag, i))
                    level_copy(aqk[:, p, :], b_l[half], 1, l, half).then_inc(qcopy, 1)
                if s[0] == "G":
                    l, half = level(s)
                    h, _ = halves(l)
                    if l == 0:
                        dve.wait_ge(xcopy, upto(xcopy, i, half + 1))
                        lost = first(xb[:, 0, cols(half)], 0)
                    else:
                        dve.wait_ge(gprod, upto(gprod, i, 2 * l - 1 + half))
                        lost = b_g[half][:, 0:256].rearrange("p (n t) -> p n t", t=h)
                    if l < LEVELS - 1:
                        part = first(gm[:, cols(half)], l)
                        V.tensor_tensor(part, part, lost, ALU.subtract).then_inc(gsub, 1)
                    else:
                        part = second(gmt[:, p, cols(half)], l)
                        V.tensor_tensor(part, part, lost, ALU.subtract).then_inc(tlast, 1)
                if s[0] == "C":
                    c = int(s[1])
                    if s[2] == "r":
                        dve.wait_ge(rprod, upto(rprod, i, c))
                        V.tensor_tensor(rt[:], chunk(vs[:, p, :], c), b_c[:, 0:P], ALU.subtract).then_inc(rsub, 1)
                    if s[2] == "s":
                        dve.wait_ge(sprod, upto(sprod, i, c + 1))
                        dve.wait_ge(oprod, upto(oprod, i - 1))
                        if c == 0:
                            V.tensor_copy(st[:, 1, :], b_c[:, 0:P]).then_inc(snew, 1)
                        else:
                            V.scalar_tensor_tensor(st[:, c + 1, :], st[:, c, :], etot[:, c:c + 1], b_c[:, 0:P],
                                                   ALU.mult, ALU.add).then_inc(snew, 1)
                if s[0] == "R":
                    half = other(s)
                    dve.wait_ge(orstd, upto(orstd, i, half + 1))
                    V.tensor_tensor(osb[:, cols(half)], osb[:, cols(half)], o2[:, cols(half)], ALU.mult).then_inc(ogate, 1)
                    dve.wait_ge(ogate, upto(ogate, i, 2 * half + 1))
                    dve.wait_ge(gact, upto(gact, i))
                    V.scalar_tensor_tensor(osb[:, cols(half)], gt[:, p, cols(half)], 1.0, osb[:, cols(half)],
                                           ALU.add, ALU.mult).then_inc(ogate, 1)
                if s[0] == "W":
                    half = other(s)
                    dve.wait_ge(cleared, 1)
                    dve.wait_ge(wo, upto(wo, i, half + 1))
                    acc = s_acc[:, bass.ds((i // H1) * T + half * HALF, HALF)]
                    V.tensor_tensor(acc, acc, b_o[half][:], ALU.add).then_inc(sacc, 1)

            turns(dve, step)

        @block.gpsimd
        def _(pool):
            G = nc.gpsimd
            G.memset(akk[:], 0.0)
            G.memset(xb[:], 0.0).then_inc(init_done, 1)
            G.memset(s_acc, 0.0).then_inc(cleared, 1)
            pool.wait_ge(init_done, 3)
            eye = ident.unsqueeze(1).to_broadcast([P, CH, P])

            def step(s, i, p):
                if s == "E":
                    pool.wait_ge(tln, upto(tln, i))
                    pool.wait_ge(wcorr, upto(wcorr, i))
                    G.tensor_tensor(al[:], al[:], aw[:], ALU.add).then_inc(splus, 1)
                    pool.wait_ge(splus, upto(splus, i, 1))
                    pool.wait_ge(evac, upto(evac, i, 2))
                    G.tensor_tensor(al[:], al[:], ar[:], ALU.add).then_inc(splus, 1)
                if s == "Sq":
                    pool.wait_ge(silu, upto(silu, i, 2))
                    pool.wait_ge(splus, upto(splus, i))
                    G.tensor_tensor(ar[:], cq[:], ks[:, p, :], ALU.mult).then_inc(qk, 1)
                if s == "M3":
                    pool.wait_ge(stat, upto(stat, i, 1))
                    pool.wait_ge(vsd, upto(vsd, i - 1))
                    G.tensor_tensor(small[:, 3, :], small[:, 0, :], halfc[:], ALU.pow).then_inc(knorm, 1)
                if s == "J":
                    pool.wait_ge(stat, upto(stat, i))
                    pool.wait_ge(gsub, upto(gsub, i - 1, 2))
                    G.tensor_tensor(mg[:].rearrange("p (g v) -> p g v", v=64),
                                    masks_x[:, 0, :].unsqueeze(1).to_broadcast([P, CH, 64]),
                                    gam[:].unsqueeze(2).to_broadcast([P, CH, 64]), ALU.mult).then_inc(mginit, 1)
                    pool.wait_ge(dprod, upto(dprod, i - 2))
                    G.tensor_tensor(gmt[:, p, :].rearrange("p (g v) -> p g v", v=P), eye, each(gam[:], P),
                                    ALU.mult).then_inc(tinit, 1)
                    pool.wait_ge(oprod, upto(oprod, i - 2))
                    G.tensor_tensor(aqk[:, p, :].rearrange("p (g v) -> p g v", v=P), eye, each(small[:, 1, :], P),
                                    ALU.mult).then_inc(diag, 1)
                if s[0] == "O":
                    half = other(s)
                    pool.wait_ge(osq, upto(osq, i, half + 1))
                    G.tensor_tensor(o2[:, cols(half)], o2[:, cols(half)], q2[:, p, cols(half)], ALU.add).then_inc(oq2, 1)
                if s[0] == "L" and s[2] == "b":
                    l, _ = level(s)
                    h, n = halves(l)
                    lo = T - 2 * (T >> l)
                    d = (dec[:, lo:lo + (T >> l)] if l else al[:]).rearrange("p (n two) -> p n two", two=2)
                    ahead, behind = d[:, :, 0], d[:, :, 1]
                    pool.wait_ge(lprod, upto(lprod, i, 2 * l + 2))
                    for t in range(2):
                        x = second(kq[:, p, t, :], l)
                        G.tensor_tensor(x, x, each(ahead, h), ALU.mult).then_inc(lup, 1)
                    x = first(ks[:, p, :], l)
                    G.tensor_tensor(x, x, each(behind, h), ALU.mult).then_inc(lup, 1)
                    if l == LEVELS - 1:
                        pool.wait_ge(snew, upto(snew, i - 1))
                    up = etot[:] if l == LEVELS - 1 else dec[:, lo + (T >> l):lo + (T >> l) + n]
                    G.tensor_tensor(up, ahead, behind, ALU.mult).then_inc(lup, 1)
                    pool.wait_ge(lup, upto(lup, i, 4 * l + 4))

            turns(pool, step)


FF = 352
FC = 3
QB = 16
FP4_STEPS = 17
MIDS = (0.25, 0.75, 1.25, 1.75, 2.5, 3.5, 5.0)
LN_EPS = 1e-5
GROUPS = B * T // HALF
E1, F1 = 4, 4


def fchunk(c):
    return min(P, FF - c * P)


def turns(eng, front, back):
    front(0, 0, 0)
    front(1, 1, 0)
    back(0, 0, 0)
    with eng.Fori(0, GROUPS // 2 - 1) as j:
        front(2 * j + 2, 0, j + 1)
        back(2 * j + 1, 1, j)
        front(2 * j + 3, 1, j + 1)
        back(2 * j + 2, 0, j + 1)
    back(GROUPS - 1, 1, GROUPS // 2 - 1)


def fp4(nc, dve, steps, before, x, rows, out, amax, scale, inv, y, m, acc, halfway=None):
    V = nc.vector
    cols = x.shape[1]
    nb = cols // QB
    blocks = lambda ap: ap.rearrange("p (n t) -> p n t", t=QB)
    each16 = lambda ap: ap[0:rows, 0:nb].unsqueeze(2).to_broadcast([rows, nb, QB])
    y, m, acc = (a[0:rows, 0:cols] for a in (y, m, acc))
    V.tensor_reduce(amax[0:rows, 0:nb], blocks(x), mybir.AxisListType.X, ALU.max,
                    apply_absolute_value=True).then_inc(steps, 1)
    dve.wait_ge(steps, before + 1)
    V.tensor_scalar(scale[0:rows, 0:nb], amax[0:rows, 0:nb], 1.0 / 6.0, 1e-12, ALU.mult, ALU.max).then_inc(steps, 1)
    dve.wait_ge(steps, before + 2)
    V.reciprocal(inv[0:rows, 0:nb], scale[0:rows, 0:nb]).then_inc(steps, 1)
    dve.wait_ge(steps, before + 3)
    V.tensor_tensor(blocks(out), blocks(x), each16(inv), ALU.mult).then_inc(steps, 1)
    V.tensor_scalar(scale[0:rows, 0:nb], scale[0:rows, 0:nb], 0.5, None, ALU.mult).then_inc(steps, 1)
    dve.wait_ge(steps, before + 4)
    V.tensor_scalar(y.bitcast(U32), out.bitcast(U32), 0x7FFFFFFF, None, ALU.bitwise_and).then_inc(steps, 1)
    dve.wait_ge(steps, before + 6)
    V.tensor_scalar(m, y, MIDS[6], None, ALU.is_gt).then_inc(steps, 1)
    V.tensor_scalar(acc, y, MIDS[5], None, ALU.is_gt).then_inc(steps, 1)
    dve.wait_ge(steps, before + 8)
    V.scalar_tensor_tensor(acc, m, 2.0, acc, ALU.mult, ALU.add).then_inc(steps, 1)
    dve.wait_ge(steps, before + 9)
    V.scalar_tensor_tensor(acc, y, MIDS[4], acc, ALU.is_gt, ALU.add).then_inc(steps, 1)
    V.tensor_scalar(m, y, MIDS[3], None, ALU.is_gt).then_inc(steps, 1)
    if halfway:
        halfway()
    dve.wait_ge(steps, before + 11)
    V.scalar_tensor_tensor(acc, acc, 2.0, m, ALU.mult, ALU.add).then_inc(steps, 1)
    for n in (2, 1, 0):
        dve.wait_ge(steps, before + 14 - n)
        V.scalar_tensor_tensor(acc, y, MIDS[n], acc, ALU.is_gt, ALU.add).then_inc(steps, 1)
    dve.wait_ge(steps, before + 15)
    V.scalar_tensor_tensor(acc.bitcast(U32), out.bitcast(U32), 0x80000000, acc.bitcast(U32),
                           ALU.bitwise_and, ALU.bitwise_or).then_inc(steps, 1)
    dve.wait_ge(steps, before + 16)
    V.tensor_tensor(blocks(out), blocks(acc), each16(scale), ALU.mult).then_inc(steps, 1)


def prepare(nc, A, c):
    with ExitStack() as ctx:
        def sb(name, shape, dt=F32):
            return ctx.enter_context(nc.sbuf_tensor(name, shape, dt))

        def sem(name):
            return ctx.enter_context(nc.semaphore(name))

        packs = sb("packs", [P, H1, PACK])
        wfa, wga = sb("wfa", [P, P]), sb("wga", [P, P])
        wfb, wgb = sb("wfb", [P, H1 * P]), sb("wgb", [P, H1 * P])
        onw = sb("onw", [P, 1])
        alog = sb("alog", [P, H1])
        dtb = sb("dtb", [P, H1])
        wnat = sb("wnat", [P, 2, FC, P])
        wdn = sb("wdn", [P, FF])
        k_t, v_t, r_t, o_t = (sb(n, [P, P]) for n in ("k_t", "v_t", "r_t", "o_t"))
        mix, mix1 = sb("mix", [P, 3]), sb("mix1", [P, 3])
        edecay = sb("edecay", [P, 1])
        dcy = sb("dcy", [P, 1])
        lng, lnb = sb("lng", [P, 1]), sb("lnb", [P, 1])
        amax, scale, inv = (sb(n, [P, 32]) for n in ("w_amax", "w_scale", "w_inv"))
        y, m, acc = (sb(n, [P, FF]) for n in ("w_y", "w_m", "w_acc"))
        pp = ctx.enter_context(nc.psum_tensor("pp", [P, 8, HALF], F32))
        s_in, s_mm, s_act, s_dve, s_out, s_fp4, s_exp, s_chain = (
            sem("w_" + n) for n in ("in", "mm", "act", "dve", "out", "fp4", "exp", "chain"))

        loads = [
            (c["ident"][:], A["ident"]), (c["ones_mean"][:], A["ones_mean"]), (c["center"][:], A["center"]),
            (c["masks_a"][:], A["masks_a"]), (c["masks_x"][:], A["masks_x"]),
            (packs[:, :, W_K:W_K + P], A["wk_t"]), (packs[:, :, W_Q:W_Q + P], A["wq_t"]),
            (packs[:, :, W_V:W_V + P], A["wv_t"]), (packs[:, :, W_O:W_O + P], A["wo_t"]),
            (packs[:, :, W_TAPS:W_TAPS + 3 * TAPS], A["taps"]), (dtb[:], A["dt"]),
            (wfa[:], A["wfa"]), (wga[:], A["wga"]), (wfb[:], A["wfb_t"]), (wgb[:], A["wgb_t"]),
            (onw[:], A["onw"]), (alog[:], A["alog"]),
            (wdn[:], A["w_down"]), (k_t[:], A["k_t"]), (v_t[:], A["v_t"]), (r_t[:], A["r_t"]), (o_t[:], A["o_t"]),
            (mix[:], A["mix"]), (dcy[:], A["decay"]), (c["tfirst"][:], A["tfirst"]), (lng[:], A["lng"]), (lnb[:], A["lnb"]),
            (c["wb_t"][:], A["wb_t"]),
        ]
        for n, w in enumerate(("w_gate", "w_up")):
            loads.append((wnat[:, n, 0:2, :], A[w][0:2 * P, :].rearrange("(c p) k -> p c k", p=P)))
            loads.append((wnat[0:fchunk(2), n, 2, :], A[w][2 * P:FF, :]))

        block = ctx.enter_context(nc.Block())

        @block.sync
        def _(sp):
            for dst, src in loads:
                sp.dma_start(dst, src).then_inc(s_in, 16)
            sp.wait_ge(s_act, 5)
            sp.wait_ge(s_dve, 3)
            sp.dma_start(A["wscr"].rearrange("h p w -> p h w"), packs[:]).then_inc(s_out, 16)
            sp.wait_ge(s_out, 16)

        @block.tensor
        def _(pe):
            pe.wait_ge(s_in, 16 * len(loads))
            for n, (wa, wb) in enumerate(((wfa, wfb), (wga, wgb))):
                for half in range(2):
                    pe.matmul(pp[:, 2 * n + half, :], wa[:], wb[:, half * HALF:(half + 1) * HALF],
                              start=True, stop=True).then_inc(s_mm, 1)
            pe.matmul(pp[:, 4, 0:1], o_t[:], lnb[:], start=True, stop=True).then_inc(s_mm, 1)
            pe.wait_ge(s_fp4, 1)
            for n in range(2):
                for ch in range(FC):
                    k = fchunk(ch)
                    pe.transpose(pp[:, 5 + n, ch * P:ch * P + k], wnat[0:k, n, ch, :], c["ident"][0:k, 0:k])
            for ch in range(FC):
                k = fchunk(ch)
                last = pe.transpose(pp[0:k, 7, ch * P:(ch + 1) * P], wdn[:, ch * P:ch * P + k], c["ident"][:])
            last.then_inc(s_mm, 1)

        @block.scalar
        def _(act):
            S = act.activation
            act.wait_ge(s_in, 16 * len(loads))
            S(alog[:], alog[:], ACT.Exp).then_inc(s_exp, 1)
            S(edecay[:], dcy[:], ACT.Exp).then_inc(s_exp, 1)
            for n, col in enumerate((W_A, W_G)):
                for half in range(2):
                    act.wait_ge(s_mm, 2 * n + half + 1)
                    S(packs[:, 4 * half:4 * half + 4, col:col + P],
                      pp[:, 2 * n + half, :].rearrange("p (h k) -> p h k", k=P), ACT.Copy).then_inc(s_act, 1)
            act.wait_ge(s_mm, 5)
            S(c["l0_bias"][:], pp[:, 4, 0:1], ACT.Copy).then_inc(s_act, 1)
            act.wait_ge(s_mm, 6)
            S(c["wgq"][:], pp[:, 5, 0:FF], ACT.Copy).then_inc(s_act, 1)
            S(c["wuq"][:], pp[:, 6, 0:FF], ACT.Copy).then_inc(s_act, 1)
            for ch in range(FC):
                k = fchunk(ch)
                S(c["wdq"][0:k, ch, :], pp[0:k, 7, ch * P:(ch + 1) * P], ACT.Copy).then_inc(s_act, 1)

        @block.vector
        def _(dve):
            V = dve
            V.memset(c["dec0"][:], 1.0).then_inc(s_chain, 1)
            V.memset(packs[:, :, W_NEGA + 1:W_O], 0.0).then_inc(s_chain, 1)
            dve.wait_ge(s_in, 16 * len(loads))
            V.tensor_scalar(onw[:], onw[:], 0.5, None, ALU.mult).then_inc(s_chain, 1)
            dve.wait_ge(s_chain, 3)
            V.tensor_scalar(packs[:, :, W_O:W_O + P], packs[:, :, W_O:W_O + P], onw[:, 0:1], None, ALU.mult).then_inc(s_dve, 1)
            V.tensor_copy(packs[:, :, W_DT:W_DT + 1], dtb[:].unsqueeze(2)).then_inc(s_dve, 1)
            dve.wait_ge(s_exp, 2)
            V.tensor_scalar(packs[:, :, W_NEGA:W_NEGA + 1], alog[:].unsqueeze(2), -1.0, None, ALU.mult).then_inc(s_dve, 1)
            V.tensor_scalar(c["dec0"][:], c["dec0"][:], edecay[:, 0:1], None, ALU.mult).then_inc(s_dve, 1)
            V.tensor_scalar(mix1[:], mix[:], -1.0, 1.0, ALU.mult, ALU.add).then_inc(s_chain, 1)
            dve.wait_ge(s_chain, 4)
            for n, w in enumerate((k_t, v_t, r_t)):
                V.tensor_scalar(c["wmix"][:, n, 0, :], w[:], mix[:, n:n + 1], None, ALU.mult).then_inc(s_dve, 1)
                V.tensor_scalar(c["wmix"][:, n, 1, :], w[:], mix1[:, n:n + 1], None, ALU.mult).then_inc(s_dve, 1)
            V.tensor_scalar(c["wo0"][:], o_t[:], lng[:, 0:1], None, ALU.mult).then_inc(s_dve, 1)
            for n in range(2):
                rows2 = wnat[:, n, 0:2, :].rearrange("p c k -> p (c k)")
                rows1 = wnat[0:fchunk(2), n, 2, :]
                dve.wait_ge(s_chain, 4 + 2 * n * FP4_STEPS)
                fp4(nc, dve, s_chain, 4 + 2 * n * FP4_STEPS, rows2, P, rows2, amax, scale, inv, y, m, acc)
                dve.wait_ge(s_chain, 4 + (2 * n + 1) * FP4_STEPS)
                fp4(nc, dve, s_chain, 4 + (2 * n + 1) * FP4_STEPS, rows1, fchunk(2), rows1, amax, scale, inv, y, m, acc)
            dve.wait_ge(s_chain, 4 + 4 * FP4_STEPS)
            fp4(nc, dve, s_chain, 4 + 4 * FP4_STEPS, wdn[:], P, wdn[:], amax, scale, inv, y, m, acc)
            dve.wait_ge(s_chain, 4 + 5 * FP4_STEPS)
            dve.sem_inc(s_fp4, 1)


def l0_feed_forward(nc, A, c, xn, g0):
    with ExitStack() as ctx:
        def sb(name, shape, dt=F32):
            return ctx.enter_context(nc.sbuf_tensor(name, shape, dt))

        xt = sb("xt", [P, 2, 4, P])
        stats = sb("stats", [P, 4, 6])
        mv = sb("mv", [P, 4, 2])
        rstd = sb("rstd", [P, 4])
        veps = sb("veps", [P, 4])
        power = sb("power", [P, 4])
        xnt = sb("xnt", [P, HALF])
        xq = sb("xq", [P, HALF])
        xqt = sb("xqt", [P, HALF])
        gs = sb("gs", [P, 2, FF])
        hid = sb("hid", [P, 2, 4 * FF])
        hqt = sb("hqt", [P, FC, HALF])
        amax, scale, inv = (sb(n, [P, 4 * FF // QB]) for n in ("f_amax", "f_scale", "f_inv"))
        y, m, acc = (sb(n, [P, 4 * FF]) for n in ("f_y", "f_m", "f_acc"))
        pt = ctx.enter_context(nc.psum_tensor("pt", [P, HALF], F32))
        pd = ctx.enter_context(nc.psum_tensor("pd", [P, HALF], F32))
        pgu = ctx.enter_context(nc.psum_tensor("pgu", [P, 4, HALF], F32))
        ph = ctx.enter_context(nc.psum_tensor("ph", [P, 2, HALF], F32))

        counters = Counters(nc, ctx)
        sem, upto = counters.sem, counters.upto

        x_in = [sem(f"f_in{p}", 16) for p in range(2)]
        ready = sem("f_ready", 0)
        passed = sem("f_passed", 0)
        bn = sem("f_bn", 8)
        var = sem("f_var", 1)
        rs = sem("f_rs", 1)
        norm = sem("f_norm", 4)
        turned = sem("f_turned", 2)
        copied = sem("f_copied", 2)
        xrounded = sem("f_xr", 1)
        gate = sem("f_gate", 4)
        silu = sem("f_silu", 4)
        mul = sem("f_mul", 4)
        hrounded = sem("f_hr", 1)
        hturned = sem("f_ht", FC)
        hcopied = sem("f_hc", FC)
        down = sem("f_down", 1)
        out = sem("f_out", 1)
        chain_x = sem("f_chain_x", FP4_STEPS)
        chain_h = sem("f_chain_h", FP4_STEPS)

        block = ctx.enter_context(nc.Block())

        @block.sync
        def _(sp):
            counters.start(sp)
            x = A["x"].rearrange("(i t p) k -> i p t k", t=4, p=P)

            def load(i, p):
                sp.wait_ge(norm, upto(norm, i - 2))
                sp.dma_start(xt[:, p], x[i]).then_inc(x_in[p], 16)
            load(0, 0)
            load(1, 1)
            with sp.Fori(0, GROUPS // 2 - 1) as j:
                load(2 * j + 2, 0)
                load(2 * j + 3, 1)

        @block.tensor
        def _(pe):
            def front(i, p, b):
                for n, (src, when) in enumerate(((xnt, norm), (xq, xrounded))):
                    pe.wait_ge(when, upto(when, i))
                    pe.wait_ge(copied, upto(copied, i, n))
                    for t in range(4):
                        last = pe.transpose(pt[:, t * P:(t + 1) * P], src[:, t * P:(t + 1) * P], c["ident"][:])
                    last.then_inc(turned, 1)
                pe.wait_ge(copied, upto(copied, i))
                for t in range(4):
                    pe.wait_ge(mul, upto(mul, i, t - 1))
                    for n, w in enumerate(("wgq", "wuq")):
                        last = pe.matmul(pgu[:, 2 * (t % 2) + n, 0:FF], xqt[:, t * P:(t + 1) * P], c[w][:],
                                         start=True, stop=True)
                    last.then_inc(gate, 1)

            def back(i, p, b):
                pe.wait_ge(hrounded, upto(hrounded, i))
                for ch in range(FC):
                    k = fchunk(ch)
                    pe.wait_ge(hcopied, upto(hcopied, i, ch - 1))
                    for t in range(4):
                        last = pe.transpose(ph[0:k, (p + ch) % 2, t * P:(t + 1) * P],
                                            hid[:, p, t * FF + ch * P:t * FF + ch * P + k], c["ident"][:])
                    last.then_inc(hturned, 1)
                pe.wait_ge(hcopied, upto(hcopied, i))
                pe.wait_ge(out, upto(out, i - 1))
                for ch in range(FC):
                    k = fchunk(ch)
                    last = pe.matmul(pd[:], c["wdq"][0:k, ch, :], hqt[0:k, ch, :], start=(ch == 0), stop=(ch == FC - 1))
                last.then_inc(down, 1)

            turns(pe, front, back)

        @block.scalar
        def _(act):
            def front(i, p, b):
                act.wait_ge(turned, upto(turned, i, 1))
                act.activation(xn[:, bass.ds(b * XS + 1 + p * HALF, HALF)], pt[:], ACT.Copy).then_inc(copied, 1)
                act.wait_ge(turned, upto(turned, i, 2))
                act.wait_ge(gate, upto(gate, i - 1))
                act.activation(xqt[:], pt[:], ACT.Copy).then_inc(copied, 1)
                for t in range(4):
                    act.wait_ge(gate, upto(gate, i, t + 1))
                    act.wait_ge(mul, upto(mul, i, t - 1))
                    act.activation(gs[:, t % 2, :], pgu[:, 2 * (t % 2), 0:FF], ACT.Silu).then_inc(silu, 1)

            def back(i, p, b):
                for ch in range(FC):
                    k = fchunk(ch)
                    act.wait_ge(hturned, upto(hturned, i, ch + 1))
                    act.wait_ge(down, upto(down, i - 1))
                    act.activation(hqt[0:k, ch, :], ph[0:k, (p + ch) % 2, :], ACT.Copy).then_inc(hcopied, 1)
                act.wait_ge(down, upto(down, i))
                act.activation(g0[:, bass.ds(b * T + p * HALF, HALF)], pd[:], ACT.Silu).then_inc(out, 1)

            turns(act, front, back)

        @block.vector
        def _(dve):
            dve.memset(power[:], -0.5).then_inc(ready, 1)
            dve.memset(xn.rearrange("p (b t) -> p b t", t=XS)[:, :, 0:1], 0.0).then_inc(ready, 1)

            def statistics(i, p, b):
                dve.wait_ge(x_in[p], upto(x_in[p], b))
                dve.wait_ge(norm, upto(norm, i - 1))
                for t in range(4):
                    dve.bn_stats(stats[:, t, :], xt[:, p, t, :]).then_inc(bn, 1)
                dve.wait_ge(bn, upto(bn, i, 4))
                dve.sem_inc(passed, 1)
                for t in range(4):
                    dve.bn_aggr(mv[:, t, :], stats[:, t, :]).then_inc(bn, 1)
                dve.wait_ge(bn, upto(bn, i))
                dve.wait_ge(rs, upto(rs, i - 1))
                dve.tensor_scalar(veps[:], mv[:, :, 1], LN_EPS, None, ALU.add).then_inc(var, 1)

            def round_x(i, p, b):
                dve.wait_ge(rs, upto(rs, i))
                dve.wait_ge(turned, upto(turned, i - 1, 1))
                for t in range(4):
                    dve.tensor_scalar(xnt[:, t * P:(t + 1) * P], xt[:, p, t, :], mv[:, t, 0:1], rstd[:, t:t + 1],
                                      ALU.subtract, ALU.mult).then_inc(norm, 1)
                dve.wait_ge(norm, upto(norm, i))
                dve.wait_ge(turned, upto(turned, i - 1))
                dve.wait_ge(chain_h, upto(chain_h, i - 2))
                fp4(nc, dve, chain_x, upto(chain_x, i - 1), xnt[:], P, xq[:], amax, scale, inv, y, m, acc)
                dve.wait_ge(chain_x, upto(chain_x, i))
                dve.sem_inc(xrounded, 1)

            def multiply(i, p, tiles):
                for t in tiles:
                    dve.wait_ge(silu, upto(silu, i, t + 1))
                    if t == 0:
                        dve.wait_ge(hturned, upto(hturned, i - 2))
                    dve.tensor_tensor(hid[:, p, t * FF:(t + 1) * FF], gs[:, t % 2, :], pgu[:, 2 * (t % 2) + 1, 0:FF],
                                      ALU.mult).then_inc(mul, 1)

            def round_hidden(i, p, halfway=None):
                dve.wait_ge(mul, upto(mul, i))
                if halfway:
                    dve.wait_ge(chain_x, upto(chain_x, i + 1))
                fp4(nc, dve, chain_h, upto(chain_h, i - 1), hid[:, p, :], P, hid[:, p, :], amax, scale, inv, y, m, acc,
                    halfway)
                dve.wait_ge(chain_h, upto(chain_h, i))
                dve.sem_inc(hrounded, 1)

            def group(i, p, b, after=True):
                round_x(i, p, b)
                round_hidden(i - 1, 1 - p, lambda: multiply(i, p, (0, 1)))
                if after:
                    statistics(i + 1, 1 - p, b + p)
                multiply(i, p, (2, 3))

            statistics(0, 0, 0)
            round_x(0, 0, 0)
            multiply(0, 0, (0, 1, 2, 3))
            statistics(1, 1, 0)
            with dve.Fori(0, GROUPS // 2 - 1) as j:
                group(2 * j + 1, 1, j)
                group(2 * j + 2, 0, j + 1)
            group(GROUPS - 1, 1, GROUPS // 2 - 1, after=False)
            round_hidden(GROUPS - 1, 1)

        @block.gpsimd
        def _(pool):
            pool.wait_ge(ready, 1)

            def front(i, p, b):
                pool.wait_ge(var, upto(var, i))
                pool.wait_ge(norm, upto(norm, i - 1))
                pool.tensor_tensor(rstd[:], veps[:], power[:], ALU.pow).then_inc(rs, 1)

            turns(pool, front, lambda i, p, b: None)


def l0_attention(nc, A, c, xn, g0, beta):
    with ExitStack() as ctx:
        def sb(name, shape, dt=F32):
            return ctx.enter_context(nc.sbuf_tensor("a_" + name, shape, dt))

        def ps(name):
            return ctx.enter_context(nc.psum_tensor("a_" + name, [P, HALF], F32))

        kc, kv, o1 = (sb(n, [P, HALF]) for n in ("kc", "kv", "o1"))
        state = sb("state", [P, 2, HALF])
        o = sb("o", [P, 2, HALF])
        sq1, r1, on = (sb(n, [P, HALF]) for n in ("sq1", "r1", "on"))
        sq2, r2 = (sb(n, [P, HALF]) for n in ("sq2", "r2"))
        xt = sb("xt", [P, 2, HALF])
        x1 = sb("x1", [P, 2, HALF])
        sg = sb("sg", [P, HALF])
        xs = sb("xs", [P, 2, HALF])
        eb = sb("eb", [P, 4 * H1])
        eps = sb("eps", [P, 1])
        pk, pv, pr, pc1, pv1, pout, pc2, pv2 = (ps(n) for n in ("pk", "pv", "pr", "pc1", "pv1", "pout", "pc2", "pv2"))

        counters = Counters(nc, ctx, "a_")
        sem, upto = counters.sem, counters.upto

        ready = sem("ready", 0)
        x_in = [sem(f"x_in{p}", 16) for p in range(2)]
        proj = sem("proj", 3)
        kcopy = sem("kcopy", 1)
        scan = sem("scan", 4)
        cen1 = sem("cen1", 1)
        sqd1 = sem("sqd1", 1)
        var1 = sem("var1", 1)
        ln1 = sem("ln1", 1)
        rsd1 = sem("rsd1", 1)
        nrm1 = sem("nrm1", 1)
        cen2, sqd2, var2, ln2, rsd2, nrm2 = (sem(n, 1) for n in ("cen2", "sqd2", "var2", "ln2", "rsd2", "nrm2"))
        outp = sem("outp", 1)
        gated = sem("gated", 1)
        x1d = sem("x1d", 1)
        x1o = [sem(f"x1o{p}", 16) for p in range(2)]
        xnc = sem("xnc", 1)
        bprod = sem("bprod", 1)
        bexp = sem("bexp", 1)
        bd = sem("bd", 2)

        def pipeline(eng, order, step):
            def turn(i, p, b, b1, b2):
                for s in order:
                    n = {"1": 1, "2": 2}.get(s[-1], 0)
                    if isinstance(i, int) and not 0 <= i - n < GROUPS:
                        continue
                    step(s, i - n, (p, 1 - p, p)[n], (b, b1, b2)[n])
            turn(0, 0, 0, 0, 0)
            turn(1, 1, 0, 0, 0)
            with eng.Fori(0, B - 1) as j:
                turn(2 * j + 2, 0, j + 1, j, j)
                turn(2 * j + 3, 1, j + 1, j + 1, j)
            turn(GROUPS, 0, B, B - 1, B - 1)
            turn(GROUPS + 1, 1, B, B, B - 1)

        block = ctx.enter_context(nc.Block())

        @block.sync
        def _(sp):
            counters.start(sp)

            def step(s, i, p, b):
                if s == "LOAD":
                    sp.wait_ge(x1d, upto(x1d, i - 2))
                    sp.dma_start(xt[:, p, :], A["x_t"][:, bass.ds(b * T + p * HALF, HALF)]).then_inc(x_in[p], 16)
                if s == "store1":
                    sp.wait_ge(x1d, upto(x1d, i))
                    sp.dma_start(A["x1scr"][:, bass.ds(b * T + p * HALF, HALF)], x1[:, p, :]).then_inc(x1o[p], 16)

            pipeline(sp, ["LOAD", "store1"], step)
            for p in range(2):
                sp.wait_ge(x1o[p], upto(x1o[p], GROUPS // 2 - 1))

        @block.tensor
        def _(pe):
            def step(s, i, p, b):
                if s in ("K", "V", "R"):
                    n = "KVR".index(s)
                    off = b * XS + 1 + p * HALF
                    if n == 0:
                        pe.wait_ge(kcopy, upto(kcopy, i - 1))
                    else:
                        pe.wait_ge(scan, upto(scan, i - 1, (0, 1, 4)[n]))
                    bank = (pk, pv, pr)[n]
                    pe.matmul(bank[:], c["wmix"][:, n, 0, :], xn[:, bass.ds(off, HALF)], start=True, stop=False)
                    pe.matmul(bank[:], c["wmix"][:, n, 1, :], xn[:, bass.ds(off - 1, HALF)],
                              start=False, stop=True).then_inc(proj, 1)
                if s == "cen1":
                    pe.wait_ge(nrm1, upto(nrm1, i - 1))
                    pe.wait_ge(scan, upto(scan, i))
                    pe.matmul(pc1[:], c["center"][:], o[:, p, :], start=True, stop=True).then_inc(cen1, 1)
                if s == "var1":
                    pe.wait_ge(ln1, upto(ln1, i - 1))
                    pe.wait_ge(sqd1, upto(sqd1, i))
                    pe.matmul(pv1[:], c["ones_mean"][:], sq1[:], start=True, stop=True).then_inc(var1, 1)
                if s == "out1":
                    pe.wait_ge(nrm1, upto(nrm1, i))
                    pe.wait_ge(gated, upto(gated, i - 1))
                    pe.matmul(pout[:], c["wo0"][:], on[:], start=True, stop=True).then_inc(outp, 1)
                if s == "cen2":
                    pe.wait_ge(nrm2, upto(nrm2, i - 1))
                    pe.wait_ge(x1d, upto(x1d, i))
                    pe.matmul(pc2[:], c["center"][:], x1[:, p, :], start=True, stop=True).then_inc(cen2, 1)
                if s == "var2":
                    pe.wait_ge(bexp, upto(bexp, i - 1))
                    pe.wait_ge(sqd2, upto(sqd2, i))
                    pe.matmul(pv2[:], c["ones_mean"][:], sq2[:], start=True, stop=True).then_inc(var2, 1)
                if s == "beta2":
                    pe.wait_ge(nrm2, upto(nrm2, i))
                    for t in range(4):
                        last = pe.matmul(pv2[:, t * H1:(t + 1) * H1], xs[:, p, t * P:(t + 1) * P], c["wb_t"][:],
                                         start=True, stop=True)
                    last.then_inc(bprod, 1)

            pipeline(pe, ["cen1", "cen2", "K", "var1", "var2", "V", "out1", "R", "beta2"], step)

        @block.scalar
        def _(act):
            act.preload_act_table_set("natural_log_exp_and_others")
            act.wait_ge(ready, 1)

            def step(s, i, p, b):
                if s == "K":
                    act.wait_ge(proj, upto(proj, i, 1))
                    act.wait_ge(scan, upto(scan, i - 1, 1))
                    act.activation(kc[:], pk[:], ACT.Copy).then_inc(kcopy, 1)
                if s == "sq1":
                    act.wait_ge(cen1, upto(cen1, i))
                    act.wait_ge(var1, upto(var1, i - 1))
                    act.activation(sq1[:], pc1[:], ACT.Square).then_inc(sqd1, 1)
                if s == "rstd1":
                    act.wait_ge(var1, upto(var1, i))
                    act.wait_ge(nrm1, upto(nrm1, i - 1))
                    act.activation(r1[:], pv1[:], ACT.Ln, bias=eps[:, 0:1]).then_inc(ln1, 1)
                    act.wait_ge(ln1, upto(ln1, i))
                    act.activation(r1[:], r1[:], ACT.Exp, scale=-0.5).then_inc(rsd1, 1)
                if s == "sq2":
                    act.wait_ge(cen2, upto(cen2, i))
                    act.wait_ge(var2, upto(var2, i - 1))
                    act.activation(sq2[:], pc2[:], ACT.Square).then_inc(sqd2, 1)
                if s == "rstd2":
                    act.wait_ge(var2, upto(var2, i))
                    act.wait_ge(nrm2, upto(nrm2, i - 1))
                    act.activation(r2[:], pv2[:], ACT.Ln, bias=eps[:, 0:1]).then_inc(ln2, 1)
                    act.wait_ge(ln2, upto(ln2, i))
                    act.activation(r2[:], r2[:], ACT.Exp, scale=-0.5).then_inc(rsd2, 1)
                if s == "xn2":
                    act.wait_ge(nrm2, upto(nrm2, i))
                    act.wait_ge(proj, upto(proj, GROUPS - 1) if isinstance(i, int) and i == GROUPS - 1 else upto(proj, i + 1))
                    act.activation(xn[:, bass.ds(b * XS + 1 + p * HALF, HALF)], xs[:, p, :], ACT.Copy).then_inc(xnc, 1)
                if s == "beta2":
                    act.wait_ge(bprod, upto(bprod, i))
                    act.wait_ge(bd, upto(bd, i - 1))
                    act.activation(eb[:], pv2[:, 0:4 * H1], ACT.Exp, scale=-1.0).then_inc(bexp, 1)

            pipeline(act, ["sq1", "sq2", "K", "rstd1", "rstd2", "xn2", "beta2"], step)

        @block.vector
        def _(dve):
            dve.memset(eps[:], LN_EPS).then_inc(ready, 1)

            def step(s, i, p, b):
                cols = bass.ds(b * T + p * HALF, HALF)
                if s == "KV":
                    dve.wait_ge(kcopy, upto(kcopy, i))
                    dve.wait_ge(proj, upto(proj, i, 2))
                    dve.wait_ge(scan, upto(scan, i - 1))
                    dve.tensor_tensor(kv[:], kc[:], pv[:], ALU.mult).then_inc(scan, 1)
                    dve.wait_ge(scan, upto(scan, i, 1))
                    dve.tensor_tensor_scan(state[:, p, :], c["dec0"][:], kv[:], state[:, 0, HALF - 1:HALF] if p else 0.0,
                                           ALU.mult, ALU.add).then_inc(scan, 1)
                    dve.wait_ge(scan, upto(scan, i, 2))
                    dve.scalar_tensor_tensor(o1[:], kv[:], c["tfirst"][:, 0:1], state[:, p, :], ALU.mult,
                                             ALU.add).then_inc(scan, 1)
                if s == "R":
                    dve.wait_ge(scan, upto(scan, i, 3))
                    dve.wait_ge(proj, upto(proj, i))
                    dve.wait_ge(cen1, upto(cen1, i - 2))
                    dve.tensor_tensor(o[:, p, :], o1[:], pr[:], ALU.mult).then_inc(scan, 1)
                if s == "norm1":
                    dve.wait_ge(rsd1, upto(rsd1, i))
                    dve.wait_ge(outp, upto(outp, i - 1))
                    dve.tensor_tensor(on[:], pc1[:], r1[:], ALU.mult).then_inc(nrm1, 1)
                if s == "x1":
                    dve.wait_ge(outp, upto(outp, i))
                    dve.wait_ge(x1d, upto(x1d, i - 1))
                    dve.scalar_tensor_tensor(sg[:], pout[:], c["l0_bias"][:, 0:1], g0[:, cols], ALU.add,
                                             ALU.mult).then_inc(gated, 1)
                    dve.wait_ge(gated, upto(gated, i))
                    dve.wait_ge(x_in[p], upto(x_in[p], b))
                    dve.wait_ge(x1o[p], upto(x1o[p], b - 1))
                    dve.wait_ge(cen2, upto(cen2, i - 2))
                    dve.tensor_tensor(x1[:, p, :], sg[:], xt[:, p, :], ALU.add).then_inc(x1d, 1)
                if s == "norm2":
                    dve.wait_ge(rsd2, upto(rsd2, i))
                    dve.wait_ge(bprod, upto(bprod, i - 2))
                    dve.wait_ge(xnc, upto(xnc, i - 2))
                    dve.tensor_tensor(xs[:, p, :], pc2[:], r2[:], ALU.mult).then_inc(nrm2, 1)
                if s == "beta2":
                    dve.wait_ge(bexp, upto(bexp, i))
                    dve.tensor_scalar(eb[:], eb[:], 1.0, None, ALU.add).then_inc(bd, 1)
                    dve.wait_ge(bd, upto(bd, i, 1))
                    dst = beta.rearrange("p (b h g) -> p b h g", h=H1, g=CH)[:, bass.ds(b, 1), :, 4 * p:4 * p + 4]
                    dve.reciprocal(dst.rearrange("p o h g -> p (o h) g"),
                                   eb[:].rearrange("p (g h) -> p h g", h=H1)).then_inc(bd, 1)

            pipeline(dve, ["norm1", "norm2", "KV", "x1", "R", "beta2"], step)


def experts(nc, A, c, xn):
    with ExitStack() as ctx:
        def sb(name, shape, dt=F32):
            return ctx.enter_context(nc.sbuf_tensor("e_" + name, shape, dt))

        counters = Counters(nc, ctx, "e_")
        sem, upto = counters.sem, counters.upto

        w1 = sb("w1", [P, E1, F1 * P])
        w2 = sb("w2", [P, E1, F1, P])
        b1 = sb("b1", [P, E1, F1])
        b2 = sb("b2", [P, E1])
        wg = sb("wg", [P, E1, P])
        bg = sb("bg", [P, E1])
        hb = sb("hb", [P, 2, HALF])
        yb = sb("yb", [P, E1, HALF])
        lb = sb("lb", [P, E1, HALF])
        above = sb("above", [P, 3, HALF], U32)
        ph = [ctx.enter_context(nc.psum_tensor(f"e_ph{n}", [P, HALF], F32)) for n in range(2)]
        py = [ctx.enter_context(nc.psum_tensor(f"e_py{n}", [P, HALF], F32)) for n in range(2)]
        pl = [ctx.enter_context(nc.psum_tensor(f"e_pl{n}", [P, HALF], F32)) for n in range(2)]
        loads = [(w1, "w1"), (w2, "w2"), (b1, "b1"), (b2, "b2"), (wg, "wg"), (bg, "bg")]

        w_in = sem("w_in", 0)
        xn_out = sem("xn_out", 0)
        up = sem("up", 16)
        gelu = sem("gelu", 16)
        down = sem("down", 16)
        yv = sem("yv", 4)
        lprod = sem("lprod", 4)
        lv = sem("lv", 4)
        sel = sem("sel", 8)
        passed = sem("passed", 0)
        stored = sem("stored", 16)

        def sequence(eng, step):
            step(0, 0, 0)
            step(1, 1, 0)
            with eng.Fori(0, B - 1) as j:
                step(2 * j + 2, 0, j + 1)
                step(2 * j + 3, 1, j + 1)

        block = ctx.enter_context(nc.Block())

        @block.sync
        def _(sp):
            counters.start(sp)
            for dst, name in loads:
                sp.dma_start(dst[:], A[name]).then_inc(w_in, 16)
            sp.dma_start(A["xnscr"].rearrange("p (b t) -> p b t", t=T),
                         xn.rearrange("p (b t) -> p b t", t=XS)[:, :, 1:XS]).then_inc(xn_out, 16)

            def step(i, p, b):
                sp.wait_ge(sel, upto(sel, i))
                sp.dma_start(A["yscr"][:, bass.ds(b * T + p * HALF, HALF)], yb[:, 0, :]).then_inc(stored, 16)

            sequence(sp, step)
            sp.wait_ge(stored, upto(stored, GROUPS - 1))
            sp.wait_ge(xn_out, 16)

        @block.tensor
        def _(pe):
            pe.wait_ge(w_in, 16 * len(loads))

            def step(i, p, b):
                x = xn[:, bass.ds(b * XS + 1 + p * HALF, HALF)]

                def part(k):
                    e, f = divmod(k, F1)
                    pe.wait_ge(gelu, upto(gelu, i, k + 1))
                    if f == 0:
                        pe.wait_ge(yv, upto(yv, i, e - 1))
                    pe.matmul(py[e % 2][:], w2[:, e, f, :], hb[:, k % 2, :], start=(f == 0),
                              stop=(f == F1 - 1)).then_inc(down, 1)

                for k in range(E1 * F1):
                    e, f = divmod(k, F1)
                    pe.wait_ge(gelu, upto(gelu, i, k - 1))
                    pe.matmul(ph[k % 2][:], w1[:, e, f * P:(f + 1) * P], x, start=True, stop=True).then_inc(up, 1)
                    if k:
                        part(k - 1)
                for e in range(E1):
                    pe.wait_ge(lv, upto(lv, i, e - 1))
                    pe.matmul(pl[e % 2][:], wg[:, e, :], x, start=True, stop=True).then_inc(lprod, 1)
                part(E1 * F1 - 1)

            sequence(pe, step)

        @block.scalar
        def _(act):
            act.wait_ge(w_in, 16 * len(loads))

            def step(i, p, b):
                def output(e):
                    act.wait_ge(down, upto(down, i, F1 * (e + 1)))
                    if e == 0:
                        act.wait_ge(stored, upto(stored, i - 1))
                    act.activation(yb[:, e, :], py[e % 2][:], ACT.Identity, bias=b2[:, e:e + 1]).then_inc(yv, 1)

                for k in range(E1 * F1):
                    e, f = divmod(k, F1)
                    act.wait_ge(up, upto(up, i, k + 1))
                    act.wait_ge(down, upto(down, i, k - 1))
                    act.activation(hb[:, k % 2, :], ph[k % 2][:], ACT.Gelu, bias=b1[:, e, f:f + 1]).then_inc(gelu, 1)
                    if f == 0 and e:
                        output(e - 1)
                for e in range(E1):
                    act.wait_ge(lprod, upto(lprod, i, e + 1))
                    act.wait_ge(sel, upto(sel, i - 1))
                    act.activation(lb[:, e, :], pl[e % 2][:], ACT.Identity, bias=bg[:, e:e + 1]).then_inc(lv, 1)
                output(E1 - 1)

            sequence(act, step)

        @block.vector
        def _(dve):
            def step(i, p, b):
                l = lambda e: lb[:, e, :]
                y = lambda e: yb[:, e, :]
                dve.wait_ge(lv, upto(lv, i))
                dve.wait_ge(sel, upto(sel, i - 1))
                dve.tensor_tensor(above[:, 0, :], l(1), l(0), ALU.is_gt).then_inc(sel, 1)
                dve.tensor_tensor(above[:, 1, :], l(3), l(2), ALU.is_gt).then_inc(sel, 1)
                dve.wait_ge(sel, upto(sel, i, 2))
                dve.tensor_tensor(l(0), l(0), l(1), ALU.max).then_inc(sel, 1)
                dve.tensor_tensor(l(2), l(2), l(3), ALU.max).then_inc(sel, 1)
                dve.wait_ge(sel, upto(sel, i, 4))
                dve.tensor_tensor(above[:, 2, :], l(2), l(0), ALU.is_gt).then_inc(sel, 1)
                dve.wait_ge(yv, upto(yv, i))
                dve.sem_inc(passed, 1)
                dve.copy_predicated(y(0), above[:, 0, :], y(1)).then_inc(sel, 1)
                dve.copy_predicated(y(2), above[:, 1, :], y(3)).then_inc(sel, 1)
                dve.wait_ge(sel, upto(sel, i, 7))
                dve.sem_inc(passed, 1)
                dve.copy_predicated(y(0), above[:, 2, :], y(2)).then_inc(sel, 1)

            sequence(dve, step)


def finish(nc, A, s1):
    with ExitStack() as ctx:
        counters = Counters(nc, ctx, "o_")
        sem, upto = counters.sem, counters.upto

        x1 = ctx.enter_context(nc.sbuf_tensor("o_x1", [P, 2, T], F32))
        y = ctx.enter_context(nc.sbuf_tensor("o_y", [P, 2, T], F32))
        x_in = [sem(f"x_in{p}", 32) for p in range(2)]
        silu = sem("silu", 1)
        mul = sem("mul", 1)
        add = sem("add", 1)
        passed = sem("passed", 0)
        out = [sem(f"out{p}", 0) for p in range(2)]
        block = ctx.enter_context(nc.Block())

        def pairs(eng, step):
            step(0, 0, 0)
            step(1, 1, 0)
            with eng.Fori(0, B // 2 - 1) as j:
                step(2 * j + 2, 0, j + 1)
                step(2 * j + 3, 1, j + 1)

        @block.sync
        def _(sp):
            counters.start(sp)

            def step(b, p, j):
                if not (isinstance(j, int) and j == 0):
                    sp.wait_ge(out[p], 16 * j)
                    sp.sem_inc(passed, 1)
                sp.dma_start(x1[:, p, :], A["x1scr"][:, bass.ds(b * T, T)]).then_inc(x_in[p], 16)
                sp.dma_start(y[:, p, :], A["yscr"][:, bass.ds(b * T, T)]).then_inc(x_in[p], 16)
            pairs(sp, step)

        @block.scalar
        def _(act):
            def step(b, p, j):
                act.wait_ge(x_in[p], upto(x_in[p], j))
                act.activation(y[:, p, :], y[:, p, :], ACT.Silu).then_inc(silu, 1)
            pairs(act, step)

        @block.vector
        def _(dve):
            def step(b, p, j):
                dve.wait_ge(silu, upto(silu, b))
                dve.tensor_tensor(y[:, p, :], y[:, p, :], s1[:, bass.ds(b * T, T)], ALU.mult).then_inc(mul, 1)
                dve.wait_ge(mul, upto(mul, b))
                dve.tensor_tensor(x1[:, p, :], x1[:, p, :], y[:, p, :], ALU.add).then_inc(add, 1)
            pairs(dve, step)

        @block.gpsimd
        def _(pool):
            def step(b, p, j):
                pool.wait_ge(add, upto(add, b))
                pool.dma_start(A["out"][:, bass.ds(b * T, T)], x1[:, p, :]).then_inc(out[p], 16)
            pairs(pool, step)
            for p in range(2):
                pool.wait_ge(out[p], 16 * (B // 2))


def build_program(nc, A):
    with ExitStack() as ctx:
        def sb(name, shape, dt=F32):
            return ctx.enter_context(nc.sbuf_tensor(name, shape, dt))

        ident, ones_mean = sb("ident", [P, P]), sb("ones_mean", [P, P])
        masks_a, masks_x = sb("masks_a", [P, LEVELS, 64]), sb("masks_x", [P, LEVELS, 64])
        beta = sb("beta", [P, B * H1 * CH])
        acc = sb("acc", [P, B * T])
        with ExitStack() as l1:
            xn = l1.enter_context(nc.sbuf_tensor("xn", [P, B * XS], F32))
            with ExitStack() as l0:
                def sb0(name, shape, dt=F32):
                    return l0.enter_context(nc.sbuf_tensor(name, shape, dt))

                c = dict(ident=ident, ones_mean=ones_mean, masks_a=masks_a, masks_x=masks_x,
                         center=sb0("center", [P, P]), wb_t=sb0("wb_t", [P, H1]), tfirst=sb0("tfirst", [P, 1]),
                         l0_bias=sb0("l0_bias", [P, 1]), dec0=sb0("dec0", [P, HALF]), wmix=sb0("wmix", [P, 3, 2, P]),
                         wo0=sb0("wo0", [P, P]), wgq=sb0("wgq", [P, FF]), wuq=sb0("wuq", [P, FF]),
                         wdq=sb0("wdq", [P, FC, P]))
                prepare(nc, A, c)
                l0_feed_forward(nc, A, c, xn[:], acc[:])
                l0_attention(nc, A, c, xn[:], acc[:], beta[:])
            experts(nc, A, c, xn[:])
        l1_attention(nc, A["xnscr"], acc[:], beta[:], ident[:], ones_mean[:], masks_a[:], masks_x[:], A["wscr"])
        finish(nc, A, acc[:])


def level_masks():
    import numpy as np

    by_column, by_row = np.zeros((2, P, LEVELS, P // 2), np.float32)
    for level in range(LEVELS):
        h = 1 << level
        token, col = np.arange(P)[:, None], np.arange(P // 2)[None, :]
        same = token // (2 * h) == col // h
        by_column[:, level] = same & (token % (2 * h) < h)
        by_row[:, level] = same & (token % (2 * h) >= h)
    return by_column, by_row


def laid_out(inputs):
    import numpy as np

    a = {k: np.asarray(v) for k, v in inputs.items()}
    p0, f0, p1, f1 = "L0_attn_", "L0_ffn_", "L1_attn_", "L1_ffn_"
    x = a[p0 + "x"].reshape(B * T, P)
    by_head = lambda w: w.reshape(H1, P, P).transpose(2, 0, 1)
    column = lambda v: v.reshape(-1, 1)
    masks_a, masks_x = level_masks()
    out = {
        "x": x, "x_t": x.T,
        "ident": np.eye(P, dtype=np.float32),
        "ones_mean": np.full((P, P), 1.0 / P, np.float32),
        "center": (np.eye(P) - np.full((P, P), 1.0 / P)).astype(np.float32),
        "masks_a": masks_a, "masks_x": masks_x,
        "mix": np.stack([a[p0 + "time_mix_" + n].reshape(P) for n in "kvr"], 1),
        "decay": column(a[p0 + "time_decay"]), "tfirst": column(a[p0 + "time_first"]),
        "k_t": a[p0 + "Wk"].T, "v_t": a[p0 + "Wv"].T, "r_t": a[p0 + "Wr"].T, "o_t": a[p0 + "Wo"].T,
        "lng": column(a[p0 + "ln_g"]), "lnb": column(a[p0 + "ln_b"]),
        "w_gate": a[f0 + "w_gate"], "w_up": a[f0 + "w_up"], "w_down": a[f0 + "w_down"],
        "wq_t": by_head(a[p1 + "Wq"]), "wk_t": by_head(a[p1 + "Wk"]), "wv_t": by_head(a[p1 + "Wv"]),
        "wo_t": a[p1 + "Wo"].reshape(P, H1, P).transpose(2, 1, 0),
        "taps": np.concatenate([a[p1 + w].reshape(H1, P, TAPS).transpose(1, 0, 2)
                                for w in ("wk_conv", "wq_conv", "wv_conv")], 2),
        "dt": a[p1 + "dt_bias"].T,
        "wfa": a[p1 + "Wfa"], "wga": a[p1 + "Wga"], "wfb_t": a[p1 + "Wfb"].T, "wgb_t": a[p1 + "Wgb"].T,
        "onw": column(a[p1 + "o_norm_w"]), "alog": np.broadcast_to(a[p1 + "A_log"], (P, H1)),
        "wb_t": a[p1 + "Wb"].T,
        "w1": a[f1 + "W1"].transpose(1, 0, 2),
        "w2": a[f1 + "W2"].reshape(E1, F1, P, P).transpose(2, 0, 1, 3),
        "b1": a[f1 + "b1"].reshape(E1, F1, P).transpose(2, 0, 1), "b2": a[f1 + "b2"].T,
        "wg": np.broadcast_to(a[f1 + "Wg"][:, :, None], (P, E1, P)), "bg": np.broadcast_to(a[f1 + "bg"], (P, E1)),
    }
    return {k: np.ascontiguousarray(v) for k, v in out.items()}


def kernel(**inputs):
    import numpy as np
    import concourse.bacc as bacc
    from concourse.bass_utils import run_bass_kernel_spmd

    nc = bacc.Bacc("TRN2", target_bir_lowering=False, num_devices=1)
    arrays, A = {}, {}
    for name, a in laid_out(inputs).items():
        arrays[f"in_{name}"] = a
        A[name] = nc.dram_tensor(f"in_{name}", a.shape, mybir.dt.from_np(a.dtype), kind="ExternalInput").ap()
    A["wscr"] = nc.dram_tensor("wscr", (H1, P, PACK), F32, kind="Internal").ap()
    A["x1scr"] = nc.dram_tensor("x1scr", (P, B * T), F32, kind="Internal").ap()
    A["xnscr"] = nc.dram_tensor("xnscr", (P, B * T), F32, kind="Internal").ap()
    A["yscr"] = nc.dram_tensor("yscr", (P, B * T), F32, kind="Internal").ap()
    A["out"] = nc.dram_tensor("out", (P, B * T), F32, kind="ExternalOutput").ap()
    build_program(nc, A)
    r = run_bass_kernel_spmd(nc, [arrays], core_ids=[0])
    return np.ascontiguousarray(r.results[0]["out"].T).reshape(B, T, P)
```
